# Optimizing a Trainium2 kernel written in Bass

```python
import numpy as np
import jax
import jax.numpy as jnp

def _softmax(x, axis=-1):
    return jax.nn.softmax(x, axis=axis)

def _gelu(x):
    return jax.nn.gelu(x, approximate=True)

def _silu(x):
    return jax.nn.silu(x)

def _sigmoid(x):
    return jax.nn.sigmoid(x)

def _layernorm(x, axis=-1, eps=1e-05):
    m = jnp.mean(x, axis=axis, keepdims=True)
    v = jnp.var(x, axis=axis, keepdims=True)
    return (x - m) / jnp.sqrt(v + eps)

def _scatter_add(tgt, idx, src, axis=0):
    return tgt.at[idx].add(src)

def _segment_sum(src, seg, n):
    return jax.ops.segment_sum(src, seg, n)
kernel_name = 'mk_xattn_seq_d1_seqx_r4_17b4b7'

def setup_inputs(seed: int=0):
    np.random.seed(seed)
    _w = jnp.asarray

    def _rec_inputs():
        import jax
        import jax.numpy as jnp
        _rk = jax.random.key(seed)
        x = -0.000719 + 1.001 * jax.random.normal(jax.random.fold_in(_rk, 1), (8, 512, 320), jnp.float32)
        _lenS = 512 - jax.random.randint(jax.random.fold_in(_rk, 7), (8,), 0, max(1, 512 // 4) + 1, jnp.int32)
        _lenS2 = 512 - jax.random.randint(jax.random.fold_in(_rk, 8), (8,), 0, max(1, 512 // 4) + 1, jnp.int32)
        _ctx_2048P = jax.random.normal(jax.random.fold_in(_rk, 11), (8, 16, 512), jnp.float32)
        _ctx_2048c = jax.random.dirichlet(jax.random.fold_in(_rk, 511), 0.3 * jnp.ones((16,), jnp.float32), (8, 512))
        _ctx_2048t = jnp.einsum('bsk,bkd->bsd', _ctx_2048c, _ctx_2048P)
        _ctx_2048t = _ctx_2048t * jax.lax.rsqrt(jnp.mean(jnp.square(_ctx_2048t)) + 1e-12) * 0.953939
        ctx_2048 = 0.00257118 + 0.99863 * (_ctx_2048t + 0.3 * jax.random.normal(jax.random.fold_in(_rk, 611), (8, 512, 512), jnp.float32))
        fside_S_0 = jax.random.uniform(jax.random.fold_in(_rk, 12), (512,), jnp.float32, 0.0, 0.999706)
        return (x, ctx_2048, fside_S_0)
    x, ctx_2048, fside_S_0 = _rec_inputs()

    def _L0_xattn_setup():
        import jax, jax.numpy as jnp
        import numpy as np
        HEADS = 20
        NUM_TOKENS = 4
        IP_SCALE = 1.0
        SEM_SCALE = 0.5
        RESCALE = 1.0
        EPS = 1e-12

        def _l2norm(x, axis=-1):
            n = jnp.sqrt(jnp.sum(x * x, axis=axis, keepdims=True))
            return x / jnp.maximum(n, EPS)
        key = jax.random.key(seed)
        ks = jax.random.split(key, 10)
        B, S, C = (2, 256, 320)
        T, E = (81, 512)
        inp = {'hidden_states': jax.random.normal(ks[0], (B, S, C), jnp.float32), 'encoder_hidden_states': jax.random.normal(ks[1], (B, T, E), jnp.float32), 'spatial_mask': jax.random.uniform(ks[2], (S,), jnp.float32), 'W_q': jax.random.normal(ks[3], (C, C), jnp.float32) * C ** (-0.5), 'W_k': jax.random.normal(ks[4], (E, C), jnp.float32) * E ** (-0.5), 'W_v': jax.random.normal(ks[5], (E, C), jnp.float32) * E ** (-0.5), 'W_k_ip': jax.random.normal(ks[6], (E, C), jnp.float32) * E ** (-0.5), 'W_v_ip': jax.random.normal(ks[7], (E, C), jnp.float32) * E ** (-0.5), 'W_out': jax.random.normal(ks[8], (C, C), jnp.float32) * C ** (-0.5), 'b_out': jnp.zeros((C,), jnp.float32)}
        return inp
    _L0_xattn_all = _L0_xattn_setup()
    _L0_xattn_in = {k: v for k, v in _L0_xattn_all.items() if k in ('W_q', 'W_k', 'W_v', 'W_k_ip', 'W_v_ip', 'W_out', 'b_out')}
    del _L0_xattn_all
    return {'x': x, 'ctx_2048': ctx_2048, 'fside_S_0': fside_S_0, 'L0_xattn_W_q': _L0_xattn_in['W_q'], 'L0_xattn_W_k': _L0_xattn_in['W_k'], 'L0_xattn_W_v': _L0_xattn_in['W_v'], 'L0_xattn_W_k_ip': _L0_xattn_in['W_k_ip'], 'L0_xattn_W_v_ip': _L0_xattn_in['W_v_ip'], 'L0_xattn_W_out': _L0_xattn_in['W_out'], 'L0_xattn_b_out': _L0_xattn_in['b_out']}

def reference(x, ctx_2048, fside_S_0, L0_xattn_W_q, L0_xattn_W_k, L0_xattn_W_v, L0_xattn_W_k_ip, L0_xattn_W_v_ip, L0_xattn_W_out, L0_xattn_b_out):
    import jax
    import jax.numpy as jnp

    def _L0_xattn_ref(hidden_states, encoder_hidden_states, spatial_mask, W_q, W_k, W_v, W_k_ip, W_v_ip, W_out, b_out):
        import jax, jax.numpy as jnp
        import numpy as np
        HEADS = 20
        NUM_TOKENS = 4
        IP_SCALE = 1.0
        SEM_SCALE = 0.5
        RESCALE = 1.0
        EPS = 1e-12

        def _l2norm(x, axis=-1):
            n = jnp.sqrt(jnp.sum(x * x, axis=axis, keepdims=True))
            return x / jnp.maximum(n, EPS)
        B, S, C = hidden_states.shape
        H = HEADS
        Dh = C // H
        attn_scale = Dh ** (-0.5)
        residual = hidden_states
        text_ehs = encoder_hidden_states[:, :-NUM_TOKENS]
        ip_ehs = encoder_hidden_states[:, -NUM_TOKENS:]

        def heads(x):
            return x.reshape(B, -1, H, Dh).transpose(0, 2, 1, 3)
        q = heads(hidden_states @ W_q)
        k_t = heads(text_ehs @ W_k)
        v_t = heads(text_ehs @ W_v)
        scores_t = jnp.einsum('bhsd,bhtd->bhst', q, k_t) * attn_scale
        probs_t = jax.nn.softmax(scores_t, axis=-1)
        text_out = jnp.einsum('bhst,bhtd->bhsd', probs_t, v_t)
        text_out = text_out.transpose(0, 2, 1, 3).reshape(B, S, C)
        k_ip = heads(ip_ehs @ W_k_ip)
        v_ip = heads(ip_ehs @ W_v_ip)
        attn_scores = jnp.einsum('bhsd,bhnd->bhsn', q, k_ip) * attn_scale
        qsem = jnp.einsum('bhst,bte->bhse', probs_t, text_ehs)
        qsem = _l2norm(qsem)
        ip_n = _l2norm(ip_ehs)
        sem = jnp.einsum('bhse,bne->bhsn', qsem, ip_n)
        sem = jax.lax.stop_gradient(sem)
        fused = attn_scores + SEM_SCALE * sem
        probs_ip = jax.nn.softmax(fused, axis=-1)
        probs_ip = probs_ip * spatial_mask[None, None, :, None]
        ip_out = jnp.einsum('bhsn,bhnd->bhsd', probs_ip, v_ip)
        ip_out = ip_out.transpose(0, 2, 1, 3).reshape(B, S, C)
        out = text_out + IP_SCALE * ip_out
        out = out @ W_out + b_out
        out = out + residual
        return out / RESCALE
    x = _L0_xattn_ref(x, ctx_2048, fside_S_0, L0_xattn_W_q, L0_xattn_W_k, L0_xattn_W_v, L0_xattn_W_k_ip, L0_xattn_W_v_ip, L0_xattn_W_out, L0_xattn_b_out)
    return x

_drawn_inputs = setup_inputs


def setup_inputs(seed=0):
    import zlib

    import numpy as np

    out = dict(_drawn_inputs(seed))
    spreads = {'L0_xattn_b_out': (0.0, 0.1)}
    factors = {}
    for name, (base, spread) in spreads.items():
        noise = np.random.default_rng([zlib.crc32(name.encode()), seed]).standard_normal(out[name].shape)
        drawn = base * np.exp(spread * noise) if base else spread * noise
        out[name] = jnp.asarray(drawn.astype(out[name].dtype))
    for name, factor in factors.items():
        out[name] = (out[name] * factor).astype(out[name].dtype)
    return out
```

```python
import concourse.bass as bass
from concourse import mybir
from contextlib import ExitStack


def xattn_kernel(
    nc: bass.Bass,
    x: bass.AP,
    ctx: bass.AP,
    spatial_mask: bass.AP,
    w_q: bass.AP,
    w_k: bass.AP,
    w_v: bass.AP,
    w_k_ip: bass.AP,
    w_v_ip: bass.AP,
    w_out: bass.AP,
    b_out: bass.AP,
    out: bass.AP,
):
    fp32 = mybir.dt.float32
    fp16 = mybir.dt.float16
    bf16 = mybir.dt.bfloat16
    ALU = mybir.AluOpType
    ACT = mybir.ActivationFunctionType
    AX = mybir.AxisListType

    B, S, C = x.shape
    E = ctx.shape[2]
    N_IP = 4
    T = ctx.shape[1] - N_IP
    H = 20
    D = C // H
    SCALE = float(D) ** -0.5
    SEM_SCALE = 0.5
    EPS = 1e-12
    TINY = 1e-30
    P = 128
    ST = S // P
    TT = 4
    TP = T // TT
    ET = E // P
    CT = [(c, min(P, C - c)) for c in range(0, C, P)]
    NC = len(CT)
    HIP = H * N_IP
    ALLIP = B * N_IP
    PROB_SCALE = 2.0 ** 14
    GRAM_TOP = 2.0 ** 14
    VW_PART = D + N_IP
    VCOLS = 3 * VW_PART + 1
    RCOLS = VW_PART + 1
    U_COLS = [T - TP * k for k in range(TT)]
    UH = [sum(U_COLS[:k]) for k in range(TT)]
    UL = [sum(U_COLS) + sum(U_COLS[:k]) for k in range(TT)]
    U_ALL = 2 * sum(U_COLS)
    PAIRS = [(0, 0), (1, 0), (2, 0), (0, 1), (1, 1), (0, 2)]
    KS = len(PAIRS) * D
    HEADS = B * H
    UNITS = HEADS * ST
    RING = 4
    BLK = RING * ST
    BLOCKS = H // RING

    q_parts = nc.dram_tensor("q_parts", [B, 3, C, S], bf16).ap()
    k_parts = nc.dram_tensor("k_parts", [B, 3, C, T], bf16).ap()
    v_parts = nc.dram_tensor("v_parts", [B, H, TP, TT * VCOLS], bf16).ap()
    u_parts = nc.dram_tensor("u_parts", [B, TP, U_ALL], fp16).ap()

    stack = ExitStack()
    with stack:
        def sb(name, shape, dt):
            return stack.enter_context(nc.sbuf_tensor(name, shape, dt))

        def sem(name):
            return stack.enter_context(nc.semaphore(name))

        ident = sb("ident", [P, P], fp32)
        ones_row = sb("ones_row", [1, P], fp32)
        headmask = sb("headmask", [P, NC, H], fp32)
        mask_col = sb("mask_col", [P, ST], fp32)
        wq = sb("wq", [P, NC, C], fp32)
        wk = sb("wk", [P, ET, C], fp32)
        wvx = sb("wvx", [P, ET, C + ALLIP], fp32)
        wout = sb("wout", [P, NC, C], fp32)
        kip_bd = sb("kip_bd", [P, NC, B, HIP], fp32)
        ip_scores = sb("ip_scores", [P, B, H, ST, N_IP], fp32)
        vw = sb("vw", [96, B, C], fp32)
        scale = sb("scale", [P, B, 3], fp32)
        reduced = sb("reduced", [P, HEADS, ST, RCOLS], fp32)
        norms = sb("norms", [P, UNITS], fp32)
        x_sb = sb("x_sb", [P, 2, ST, C], fp32)
        u_sb = sb("u_sb", [TP, 2, U_ALL], fp16)
        v_ring = sb("v_ring", [TP, RING, TT, VCOLS], bf16)
        q_ring = sb("q_ring", [KS, RING, S], bf16)
        k_ring = sb("k_ring", [KS, RING, T], bf16)
        probs = sb("probs", [P, ST, T], fp32)
        neg_max = sb("neg_max", [P, ST], fp32)
        probs_hi = sb("probs_hi", [TP, 2, S], fp16)
        probs_lo = sb("probs_lo", [TP, 2, S], fp16)
        discard = sb("discard", [P, 2, E], fp32)
        out_raw = sb("out_raw", [P, 4, 2, VCOLS], fp32)
        v_sb = sb("v_sb", [TP, H, TT, VCOLS], bf16)
        work = sb("work", [P, 2 * NC * S], fp32)
        late = sb("late", [P, 2 * NC * 3 * S // 2], fp32)
        parts = late[:, :].bitcast(bf16).rearrange("p (t a s) -> p t a s", t=2 * NC, a=3)
        q_full = work[:, 0:NC * S].rearrange("p (c s) -> p c s", c=NC)
        resid = work[:, NC * S:2 * NC * S].rearrange("p (r s) -> p r s", r=3)
        resid_v = sb("resid_v", [TP, 2, C], fp32)
        sem_raw = sb("sem_raw", [TP, TT, N_IP], fp32)
        sem_res = sb("sem_res", [TP, 2, TT, N_IP], fp32)
        sumsq = sb("sumsq", [TP, TT], fp32)
        row_max = sb("row_max", [TP, 1], fp32)
        top = sb("top", [1, 2], fp32)
        scale_row = sb("scale_row", [1, 3], fp32)
        ip_stat = sb("ip_stat", [ALLIP, 8], fp32)
        spare = reduced[:, :, :, :].rearrange("p g s c -> p (g s c)")
        taken = [0]

        def carve(parts_n, n):
            a = spare[0:parts_n, taken[0]:taken[0] + n]
            taken[0] += n
            assert taken[0] <= HEADS * ST * RCOLS
            return a

        ctx_sb = carve(TP, TT * E).rearrange("p (k e) -> p k e", k=TT)
        ctx_t = carve(P, ET * T).rearrange("p (e t) -> p e t", e=ET)
        x_t = carve(P, NC * S).rearrange("p (c s) -> p c s", c=NC)
        wk_ip = carve(P, ET * C).rearrange("p (e c) -> p e c", e=ET)
        wv_ip = carve(P, ET * C).rearrange("p (e c) -> p e c", e=ET)
        vip_bd = carve(P, NC * B * HIP).rearrange("p (m b c) -> p m b c", m=NC, b=B)
        ip_rows = carve(ALLIP, 2 * E).rearrange("p (a e) -> p a e", a=2)
        ip_t = carve(P, ET * ALLIP).rearrange("p (e i) -> p e i", e=ET)
        NS = 2 * ST * C
        text = late[:, 0:NS].rearrange("p (a s c) -> p a s c", a=2, s=ST)
        inv_sum, inv_norm, square = (late[:, NS + n * UNITS:NS + (n + 1) * UNITS] for n in range(3))
        text_t = work[:, :].rearrange("p (a c s) -> p a c s", a=2, c=NC)
        over_probs = probs[:, :, :].rearrange("p s t -> p (s t)")
        root, root2 = (over_probs[:, n * UNITS:(n + 1) * UNITS] for n in range(2))
        fused, ip_exp = (over_probs[:, 2 * UNITS + n * ST * HIP:2 * UNITS + (n + 1) * ST * HIP] for n in range(2))
        ip_stat3 = sb("ip_stat3", [P, 2 * ST * H], fp32)
        ip_probs = sb("ip_probs", [P, 2, ST, HIP], fp32)
        ip_probs_t = sb("ip_probs_t", [96, 2, S], fp32)
        y_sb = sb("y_sb", [P, ST, C], fp32)

        bank = [stack.enter_context(nc.psum_tensor(f"bank{j}", [P, 512], fp32)) for j in range(8)]
        S_BANK, PT_BANK, Y_BANK, O_BANK = 0, 2, 4, 6

        consts_made = sem("consts_made")
        unwatched = sem("unwatched")
        ip_loaded = sem("ip_loaded")
        ip_weights_loaded = sem("ip_weights_loaded")
        weights_loaded = sem("weights_loaded")
        late_loaded = sem("late_loaded")
        ip_step = sem("ip_step")
        ip_root = sem("ip_root")
        bank_filled = [sem(f"bank_filled{j}") for j in range(8)]
        bank_drained = [sem(f"bank_drained{j}") for j in range(8)]
        x_loaded = sem("x_loaded")
        ctx_loaded = sem("ctx_loaded")
        x_reloaded = [sem(f"x_reloaded{par}") for par in range(2)]
        x_t_ready = sem("x_t_ready")
        ctx_t_ready = sem("ctx_t_ready")
        scale_step = sem("scale_step")
        sumsq_ready = sem("sumsq_ready")
        row_max_ready = sem("row_max_ready")
        scale_row_ready = sem("scale_row_ready")
        q_full_ready = sem("q_full_ready")
        hi_split = sem("hi_split")
        mid_split = sem("mid_split")
        parts_split = sem("parts_split")
        parts_saved = sem("parts_saved")
        v_hi_split = sem("v_hi_split")
        v_mid_split = sem("v_mid_split")
        v_split = sem("v_split")
        sem_step = sem("sem_step")
        u_hi_split = sem("u_hi_split")
        v_saved = sem("v_saved")
        u_saved = sem("u_saved")
        head_loaded = [sem(f"head_loaded{r}") for r in range(RING)]
        u_loaded = sem("u_loaded")
        scores_filled = sem("scores_filled")
        row_max_found = sem("row_max_found")
        probs_ready = sem("probs_ready")
        probs_t_filled = sem("probs_t_filled")
        hi_ready = sem("hi_ready")
        lo_ready = sem("lo_ready")
        quad_filled = sem("quad_filled")
        norms_done = sem("norms_done")
        out_filled = sem("out_filled")
        out_drained = sem("out_drained")
        pool_sum = sem("pool_sum")
        head_reduced = sem("head_reduced")
        norm_step = sem("norm_step")
        square_ready = sem("square_ready")
        root_ready = sem("root_ready")
        inv_sum_ready = sem("inv_sum_ready")
        elem_step = sem("elem_step")
        ip_fused = sem("ip_fused")
        ip_exp_ready = sem("ip_exp_ready")
        ip_probs_ready = sem("ip_probs_ready")
        text_ready = sem("text_ready")
        text_t_filled = sem("text_t_filled")
        text_t_ready = sem("text_t_ready")
        y_filled = sem("y_filled")
        y_ready = sem("y_ready")
        y_stored = sem("y_stored")

        SETUP_USES = [2, 2, 2, 2, 1, 1, 1, 1]
        USES = [3, 3, 3, 2, 3, 3, 3, 4]
        R1 = 3
        RV = 2
        Q_JOB = [(0, 2), (1, 2), (2, 2)]
        XT_JOB = [(0, 1), (1, 1), (2, 1)]
        CT_JOB = [(3, 1), (4, 1), (5, 1), (6, 1)]
        TOP_JOB, SCALE_JOB = (7, 1), (7, 2)
        K_JOB = [(3, 2), (4, 2), (5, 2)]
        V_JOB = [(6, 2), (7, 3), (0, 3), (1, 3)]
        IPS_JOB = (2, 3)
        G_JOB = [(4, 3), (5, 3), (6, 3), (7, 4)]

        def use(job, b):
            return SETUP_USES[job[0]] + USES[job[0]] * b + job[1]

        def end_of_phase1(j):
            return SETUP_USES[j] + USES[j] * B

        CONSTS = 8

        def apart(eng):
            eng.sem_inc(unwatched, 1)

        block = stack.enter_context(nc.Block())

        @block.sync
        def _(sp):
            for b in range(B):
                sp.dma_start(ip_rows[b * N_IP:(b + 1) * N_IP, 0, :], ctx[b, T:T + N_IP, :]).then_inc(ip_loaded, 16)
            ctx_in = ctx[:, 0:T, :].rearrange("b (k p) e -> b p k e", p=TP)
            x_in = x.rearrange("b (s p) c -> b p s c", p=P)
            sp.dma_start(x_sb[:, 0], x_in[0]).then_inc(x_loaded, 16)
            sp.dma_start(ctx_sb, ctx_in[0]).then_inc(ctx_loaded, 16)
            sp.dma_start(wk_ip, w_k_ip.rearrange("(e p) c -> p e c", p=P)).then_inc(ip_weights_loaded, 16)
            sp.dma_start(wv_ip, w_v_ip.rearrange("(e p) c -> p e c", p=P)).then_inc(ip_weights_loaded, 16)

            def store_batch(b):
                for t in range(2 * NC):
                    c0, cn = CT[t % NC]
                    sp.wait_ge(parts_split, R1 + 2 * NC * b + t + 1)
                    dst = (q_parts if t < NC else k_parts)[b, :, c0:c0 + cn, :].rearrange("a c s -> c a s")
                    n = S if t < NC else T
                    sp.dma_start(dst, parts[0:cn, t, :, 0:n]).then_inc(parts_saved, 16)
                sp.wait_ge(v_split, RV + TT * (b + 1))
                apart(sp)
                sp.wait_ge(sem_step, 5 * (b + 1))
                sp.dma_start(v_parts[b].rearrange("h p c -> p h c"), v_sb[:, :, :, :].rearrange("p h k c -> p h (k c)"))\
                  .then_inc(v_saved, 16)
                sp.wait_ge(bank_drained[G_JOB[-1][0]], use(G_JOB[-1], b))
                sp.dma_start(u_parts[b], u_sb[:, 1, :]).then_inc(u_saved, 16)

            with sp.Fori(0, B - 1) as b:
                sp.wait_ge(bank_filled[XT_JOB[-1][0]], use(XT_JOB[-1], b))
                sp.dma_start(x_sb[:, 0], x_in[b + 1]).then_inc(x_loaded, 16)
                sp.wait_ge(bank_filled[CT_JOB[-1][0]], use(CT_JOB[-1], b))
                sp.wait_ge(row_max_ready, b + 1)
                sp.dma_start(ctx_sb, ctx_in[b + 1]).then_inc(ctx_loaded, 16)
                store_batch(b)
            store_batch(B - 1)

            sp.wait_ge(parts_saved, 1 + 16 * 2 * NC * B)
            sp.wait_ge(v_saved, 1 + 16 * B)
            sp.wait_ge(u_saved, 1 + 16 * B)

            def load_u(b, par):
                sp.dma_start(u_sb[:, par, :], u_parts[b]).then_inc(u_loaded, 16)

            def load_heads(b, i, blk, free):
                for r in range(RING):
                    rows = bass.ds(i * (RING * D) + r * D, D)
                    if free:
                        sp.wait_ge(scores_filled, BLK * blk + ST * (r + 1) - BLK)
                    for a0, n in ((0, 3), (3, 2), (5, 1)):
                        sp.dma_start(q_ring[a0 * D:(a0 + n) * D, r, :], q_parts[b, 0:n, rows, :])\
                          .then_inc(head_loaded[r], 16)
                    if free:
                        sp.wait_ge(quad_filled, BLK * blk + ST * (r + 1) - BLK)
                    sp.dma_start(v_ring[:, r].rearrange("p k c -> p (k c)"), v_parts[b, bass.ds(i * RING + r, 1), :, :]
                                 .rearrange("a p c -> p (a c)")).then_inc(head_loaded[r], 16)
                    for a, (_, kp) in enumerate(PAIRS):
                        sp.dma_start(k_ring[a * D:(a + 1) * D, r, :], k_parts[b, kp, rows, :])\
                          .then_inc(head_loaded[r], 16)

            load_u(0, 0)
            load_heads(0, 0, 0, False)
            with sp.Fori(1, BLOCKS) as i:
                load_heads(0, i, i, True)
            load_u(1, 1)
            with sp.Fori(0, BLOCKS) as i:
                load_heads(1, i, BLOCKS + i, True)
            with sp.Fori(1, B // 2) as pair:
                for par in range(2):
                    sp.wait_ge(quad_filled, H * ST * (2 * pair + par - 1))
                    apart(sp)
                    load_u(2 * pair + par, par)
                    with sp.Fori(0, BLOCKS) as i:
                        load_heads(2 * pair + par, i, BLOCKS * (2 * pair + par) + i, True)

            def load_x(b, par):
                sp.dma_start(x_sb[:, par], x_in[b]).then_inc(x_reloaded[par], 16)

            out_v = out.rearrange("b (s p) c -> b p s c", p=P)

            def store_y(b):
                for s in range(ST):
                    sp.wait_ge(y_ready, ST * b + s + 1)
                    sp.dma_start(out_v[b, :, s, :], y_sb[:, s, :]).then_inc(y_stored, 16)

            sp.wait_ge(bank_filled[XT_JOB[-1][0]], use(XT_JOB[-1], B - 1))
            load_x(0, 0)
            load_x(1, 1)
            with sp.Fori(0, B // 2 - 1) as pair:
                for par in range(2):
                    store_y(2 * pair + par)
                    load_x(2 * pair + par + 2, par)
            store_y(B - 2)
            store_y(B - 1)
            sp.wait_ge(y_stored, 16 * ST * B)

        @block.gpsimd
        def _(pool):
            nc.gpsimd.memset(ident[:, :], 0.0).then_inc(consts_made, 1)
            nc.gpsimd.memset(headmask[:, :, :], 1.0).then_inc(consts_made, 1)
            nc.gpsimd.memset(ones_row[:, :], 1.0).then_inc(consts_made, 1)
            nc.gpsimd.memset(ip_probs_t[:, :, :], 1.0).then_inc(consts_made, 1)
            nc.gpsimd.memset(v_sb[:, :, :, VCOLS - 1:VCOLS], 1.0).then_inc(consts_made, 1)
            pool.wait_ge(consts_made, 5)
            nc.gpsimd.affine_select(out=ident[:, :], in_=ident[:, :], compare_op=ALU.not_equal, fill=1.0, base=0,
                                    pattern=[[-1, P]], channel_multiplier=1).then_inc(consts_made, 1)
            nc.gpsimd.affine_select(out=headmask[:, :, :], in_=headmask[:, :, :], compare_op=ALU.is_ge, fill=0.0,
                                    base=0, pattern=[[P, NC], [-D, H]], channel_multiplier=1).then_inc(consts_made, 1)
            pool.wait_ge(consts_made, 7)
            nc.gpsimd.affine_select(out=headmask[:, :, :], in_=headmask[:, :, :], compare_op=ALU.is_ge, fill=0.0,
                                    base=D - 1, pattern=[[-P, NC], [D, H]], channel_multiplier=-1)\
              .then_inc(consts_made, 1)
            pool.sem_inc(parts_split, R1)
            pool.sem_inc(v_split, RV)
            pool.sem_inc(head_reduced, 2)
            for saved in (parts_saved, v_saved, u_saved):
                pool.sem_inc(saved, 1)

            with pool.Fori(0, B) as b:
                for t in range(2 * NC):
                    j, c0, cn = (Q_JOB + K_JOB)[t], *CT[t % NC]
                    n = S if t < NC else T
                    pool.wait_ge(bank_drained[j[0]], use(j, b))
                    apart(pool)
                    nc.gpsimd.tensor_copy(parts[0:cn, t, 1, 0:n], resid[0:cn, t % R1, 0:n]).then_inc(mid_split, 1)
                    pool.wait_ge(mid_split, 2 * NC * b + t + 1)
                    nc.gpsimd.tensor_tensor(parts[0:cn, t, 2, 0:n], resid[0:cn, t % R1, 0:n], parts[0:cn, t, 1, 0:n],
                                            ALU.subtract).then_inc(parts_split, 1)
                for k in range(TT):
                    j = V_JOB[k]
                    v_k = v_sb[:, :, k, :]
                    r_k = resid_v[:, k % RV, :].rearrange("p (h d) -> p h d", d=D)
                    pool.wait_ge(bank_drained[j[0]], use(j, b))
                    apart(pool)
                    nc.gpsimd.tensor_copy(v_k[:, :, VW_PART:VW_PART + D], r_k).then_inc(v_mid_split, 1)
                    pool.wait_ge(v_mid_split, TT * b + k + 1)
                    nc.gpsimd.tensor_tensor(v_k[:, :, 2 * VW_PART:2 * VW_PART + D], r_k,
                                            v_k[:, :, VW_PART:VW_PART + D], ALU.subtract).then_inc(v_split, 1)
                pool.wait_ge(v_hi_split, TT * (b + 1))
                apart(pool)

                def sem_part(a):
                    return v_sb[:, :, :, a * VW_PART + D:(a + 1) * VW_PART]

                def to_heads(src):
                    return src.unsqueeze(1).broadcast_to([TP, H, TT, N_IP])

                src = sem_raw[:, :, :]
                for a in range(3):
                    nc.gpsimd.tensor_copy(sem_part(a), to_heads(src)).then_inc(sem_step, 1)
                    if a < 2:
                        pool.wait_ge(sem_step, 5 * b + 2 * a + 1)
                        nc.gpsimd.tensor_tensor(sem_res[:, a], src, sem_part(a)[:, 0, :, :],
                                                ALU.subtract).then_inc(sem_step, 1)
                        pool.wait_ge(sem_step, 5 * b + 2 * a + 2)
                        apart(pool)
                        src = sem_res[:, a]

            def reduce_head(g, slot):
                pool.wait_ge(out_drained, 2 + 2 * g + 2)
                apart(pool)
                raw = out_raw[:, 2 * slot:2 * slot + 2].rearrange("p a u c -> p (a u) c")
                nc.gpsimd.tensor_tensor(reduced[:, g, :, 0:VW_PART], raw[:, :, 0:VW_PART],
                                        raw[:, :, VW_PART:2 * VW_PART], ALU.add).then_inc(pool_sum, 1)
                nc.gpsimd.tensor_copy(reduced[:, g, :, VW_PART:RCOLS], raw[:, :, VCOLS - 1:VCOLS])
                pool.wait_ge(pool_sum, g + 1)
                apart(pool)
                nc.gpsimd.tensor_tensor(reduced[:, g, :, 0:VW_PART], reduced[:, g, :, 0:VW_PART],
                                        raw[:, :, 2 * VW_PART:3 * VW_PART], ALU.add).then_inc(head_reduced, 1)

            with pool.Fori(0, HEADS // 2) as g2:
                for slot in range(2):
                    reduce_head(2 * g2 + slot, slot)

            pool.wait_ge(head_reduced, 2 + HEADS)
            pool.wait_ge(inv_sum_ready, 1)

            def step(b, par, free):
                if free:
                    pool.wait_ge(text_t_filled, (NC + 1) * (b - 1))
                    apart(pool)
                red_b = reduced[:, bass.ds(b * H, H), :, 0:D]
                inv_b = inv_sum[:, bass.ds(b * (H * ST), H * ST)].rearrange("p (h s) -> p h s", s=ST)
                nc.gpsimd.tensor_tensor(text[:, par].rearrange("p s (h d) -> p h s d", d=D), red_b,
                                        inv_b.unsqueeze(3).broadcast_to([P, H, ST, D]), ALU.mult)\
                  .then_inc(text_ready, 1)

            step(0, 0, False)
            step(1, 1, False)
            with pool.Fori(1, B // 2) as pair:
                for par in range(2):
                    step(2 * pair + par, par, True)

        @block.scalar
        def _(act):
            act.dma_start(wq[:, 0:2, :], w_q[0:2 * P, :].rearrange("(m p) c -> p m c", p=P)).then_inc(weights_loaded, 16)
            act.dma_start(wq[0:CT[2][1], 2, :], w_q[2 * P:C, :]).then_inc(weights_loaded, 16)
            act.dma_start(wk[:, :, :], w_k.rearrange("(e p) c -> p e c", p=P)).then_inc(weights_loaded, 16)
            act.dma_start(wvx[:, :, 0:C], w_v.rearrange("(e p) c -> p e c", p=P)).then_inc(weights_loaded, 16)
            act.dma_start(wout[:, 0:2, :], w_out[0:2 * P, :].rearrange("(m p) c -> p m c", p=P)).then_inc(weights_loaded, 16)
            act.dma_start(wout[0:CT[2][1], 2, :], w_out[2 * P:C, :]).then_inc(weights_loaded, 16)
            act.dma_start(mask_col[:, :], spatial_mask.rearrange("(s p) -> p s", p=P), allow_slow_non_contiguous=True).then_inc(late_loaded, 16)
            for b in range(B):
                act.dma_start(vw[HIP:HIP + 1, b, :], b_out.rearrange("(a c) -> a c", a=1)).then_inc(late_loaded, 16)
            act.wait_ge(ip_step, 1)
            nc.scalar.activation(ip_stat[:, 1:2], ip_stat[:, 0:1], ACT.Sqrt).then_inc(ip_root, 1)
            act.wait_ge(bank_filled[0], 1)
            nc.scalar.activation(ip_t, bank[0][:, 0:ET * ALLIP].rearrange("p (e i) -> p e i", e=ET), ACT.Copy)\
              .then_inc(bank_drained[0], 1)
            act.wait_ge(weights_loaded, 16 * 6)
            act.wait_ge(bank_filled[1], 1)
            nc.scalar.activation(wvx[:, :, C:C + ALLIP], bank[1][:, 0:ET * ALLIP].rearrange("p (e i) -> p e i", e=ET),
                                 ACT.Copy).then_inc(bank_drained[1], 1)

            for b in range(B):
                act.wait_ge(bank_filled[b], SETUP_USES[b])
                nc.scalar.activation(vw[0:HIP, b, :], bank[b][0:HIP, 0:C], ACT.Copy).then_inc(bank_drained[b], 1)

            with act.Fori(0, B) as b:
                for c, (c0, cn) in enumerate(CT):
                    j = XT_JOB[c]
                    act.wait_ge(bank_filled[j[0]], use(j, b))
                    nc.scalar.activation(x_t[0:cn, c, :], bank[j[0]][0:cn, 0:S], ACT.Copy).then_inc(bank_drained[j[0]], 1)
                for e in range(ET):
                    j = CT_JOB[e]
                    act.wait_ge(bank_filled[j[0]], use(j, b))
                    nc.scalar.activation(ctx_t[:, e, :], bank[j[0]][:, 0:T], ACT.Copy).then_inc(bank_drained[j[0]], 1)
                act.wait_ge(parts_saved, 1 + 16 * 2 * NC * b)
                for t in range(2 * NC):
                    j, c0, cn = (Q_JOB + K_JOB)[t], *CT[t % NC]
                    act.wait_ge(bank_filled[j[0]], use(j, b))
                    if t < NC:
                        nc.scalar.activation(q_full[0:cn, t, :], bank[j[0]][0:cn, 0:S], ACT.Copy).then_inc(q_full_ready, 1)
                        nc.scalar.activation(parts[0:cn, t, 0, 0:S], bank[j[0]][0:cn, 0:S], ACT.Copy).then_inc(hi_split, 1)
                    else:
                        nc.scalar.activation(parts[0:cn, t, 0, 0:T], bank[j[0]][0:cn, 0:T], ACT.Copy, scale=SCALE)\
                          .then_inc(hi_split, 1)
                act.wait_ge(v_saved, 1 + 16 * b)
                for k in range(TT):
                    j = V_JOB[k]
                    v_k = v_sb[:, :, k, :]
                    act.wait_ge(bank_filled[j[0]], use(j, b))
                    nc.scalar.activation(v_k[:, :, 0:D], bank[j[0]][0:TP, 0:C].rearrange("p (h d) -> p h d", d=D), ACT.Copy)
                    nc.scalar.activation(sem_raw[:, k, :], bank[j[0]][0:TP, bass.ds(b * N_IP + C, N_IP)], ACT.Copy)\
                      .then_inc(v_hi_split, 1)
                act.wait_ge(bank_filled[IPS_JOB[0]], use(IPS_JOB, b))
                apart(act)
                nc.scalar.activation(ip_scores[:, b].rearrange("p h s n -> p s h n"),
                                     bank[IPS_JOB[0]][:, 0:ST * HIP].rearrange("p (s h n) -> p s h n", s=ST, n=N_IP), ACT.Copy)\
                  .then_inc(bank_drained[IPS_JOB[0]], 1)
                act.wait_ge(bank_drained[SCALE_JOB[0]], use(SCALE_JOB, b))
                act.wait_ge(u_saved, 1 + 16 * b)
                for k in range(TT):
                    j, n = G_JOB[k], U_COLS[k]
                    act.wait_ge(bank_filled[j[0]], use(j, b))
                    apart(act)
                    if n > TP:
                        nc.scalar.activation(u_sb[:, 1, UH[k] + TP:UH[k] + n], bank[j[0]][0:TP, TP:n], ACT.Identity,
                                             scale=scale[0:TP, b, 0:1])
                    nc.scalar.activation(u_sb[:, 1, UH[k]:UH[k] + TP], bank[j[0]][0:TP, 0:TP], ACT.Identity,
                                         scale=scale[0:TP, b, 1:2]).then_inc(u_hi_split, 1)

            def exp(v, st, free):
                act.wait_ge(row_max_found, v + 1)
                if free:
                    act.wait_ge(norms_done, v - 1)
                nc.scalar.activation(probs[:, st, :], bank[S_BANK + st % 2][:, 0:T], ACT.Exp, bias=neg_max[:, st:st + 1])\
                  .then_inc(probs_ready, 1)

            def hi(v, par):
                act.wait_ge(probs_t_filled, v + 1)
                nc.scalar.activation(probs_hi[:, par, :], bank[PT_BANK + par][0:TP, 0:S], ACT.Copy, scale=PROB_SCALE)\
                  .then_inc(hi_ready, 1)

            def drain_out(g, pair, slot):
                act.wait_ge(out_filled, 2 * g + pair + 1)
                act.wait_ge(head_reduced, g + 1)
                nc.scalar.activation(out_raw[:, 2 * slot + pair].rearrange("p u c -> p (u c)"),
                                     bank[O_BANK + pair][:, 0:2 * VCOLS], ACT.Copy).then_inc(out_drained, 1)

            def head_steps(g, slot, first):
                for j in range(ST):
                    exp(ST * g + j, j, not first)
                    if not (first and j == 0):
                        hi(ST * g + j - 1, (j - 1) % 2)
                    if j % 2 == 0 and not first:
                        drain_out(g - 1, j // 2, (slot - 1) % 2)

            head_steps(0, 0, True)
            head_steps(1, 1, False)
            with act.Fori(1, HEADS // 2) as g2:
                for slot in range(2):
                    head_steps(2 * g2 + slot, slot, False)
            hi(UNITS - 1, (ST - 1) % 2)
            for pair in range(2):
                drain_out(HEADS - 1, pair, 1)

            act.wait_ge(square_ready, 1)
            nc.scalar.activation(root, square, ACT.Sqrt).then_inc(root_ready, 1)

            def step(b, par):
                act.wait_ge(ip_fused, b + 1)
                nc.scalar.activation(ip_exp, fused, ACT.Exp, scale=SEM_SCALE).then_inc(ip_exp_ready, 1)
                for c, (c0, cn) in enumerate(CT):
                    act.wait_ge(text_t_filled, (NC + 1) * b + c + 1)
                    nc.scalar.activation(text_t[0:cn, par, c, :], bank[c][0:cn, 0:S], ACT.Copy).then_inc(text_t_ready, 1)
                act.wait_ge(text_t_filled, (NC + 1) * b + NC + 1)
                nc.scalar.activation(ip_probs_t[0:HIP, par, :], bank[NC][0:HIP, 0:S], ACT.Copy).then_inc(text_t_ready, 1)

            with act.Fori(0, B // 2) as pair:
                for par in range(2):
                    step(2 * pair + par, par)

        @block.vector
        def _(dve):
            dve.sem_inc(norms_done, 2)
            dve.sem_inc(out_drained, 2)
            dve.wait_ge(ip_loaded, 16 * B)
            nc.vector.scalar_tensor_tensor(discard[0:ALLIP, 0, :], ip_rows[:, 0, :], 1.0, ip_rows[:, 0, :], ALU.mult, ALU.mult,
                                           accum_out=ip_stat[:, 0:1]).then_inc(ip_step, 1)
            dve.wait_ge(ip_root, 1)
            nc.vector.tensor_scalar(ip_stat[:, 2:3], ip_stat[:, 1:2], 1e-18, None, ALU.max).then_inc(ip_step, 1)
            dve.wait_ge(ip_step, 2)
            nc.vector.reciprocal(ip_stat[:, 3:4], ip_stat[:, 2:3]).then_inc(ip_step, 1)
            dve.wait_ge(ip_step, 3)
            nc.vector.scalar_tensor_tensor(ip_stat[:, 4:5], ip_stat[:, 0:1], ip_stat[:, 3:4], ip_stat[:, 2:3], ALU.mult,
                                           ALU.add).then_inc(ip_step, 1)
            dve.wait_ge(ip_step, 4)
            nc.vector.tensor_scalar(ip_stat[:, 5:6], ip_stat[:, 4:5], 0.5, EPS, ALU.mult, ALU.max).then_inc(ip_step, 1)
            dve.wait_ge(ip_step, 5)
            nc.vector.reciprocal(ip_stat[:, 6:7], ip_stat[:, 5:6]).then_inc(ip_step, 1)
            dve.wait_ge(ip_step, 6)
            nc.vector.tensor_scalar(ip_rows[:, 1, :], ip_rows[:, 0, :], ip_stat[:, 6:7], None, ALU.mult).then_inc(ip_step, 1)
            dve.wait_ge(consts_made, CONSTS)
            for j, bd, n_last in ((2, kip_bd, 0), (3, vip_bd, 1)):
                dve.wait_ge(bank_filled[j], 1)
                for m, (c0, cn) in enumerate(CT):
                    src = bank[j][0:cn, m * ALLIP:(m + 1) * ALLIP].rearrange("p (b n) -> p b n", b=B)
                    last = nc.vector.tensor_tensor(
                        bd[0:cn, m].rearrange("p b (h n) -> p b h n", n=N_IP),
                        src.unsqueeze(2).broadcast_to([cn, B, H, N_IP]),
                        headmask[0:cn, m, :].unsqueeze(1).unsqueeze(3).broadcast_to([cn, B, H, N_IP]), ALU.mult)
                last.then_inc(bank_drained[j], 1)

            with dve.Fori(0, B) as b:
                dve.wait_ge(ctx_loaded, 16 * (b + 1))
                for k in range(TT):
                    if k >= 2:
                        dve.wait_ge(sumsq_ready, TT * b + k - 1)
                    nc.vector.scalar_tensor_tensor(discard[0:TP, k % 2, :], ctx_sb[:, k, :], 1.0, ctx_sb[:, k, :], ALU.mult, ALU.mult,
                                                   accum_out=sumsq[:, k:k + 1]).then_inc(sumsq_ready, 1)
                dve.wait_ge(sumsq_ready, TT * (b + 1))
                nc.vector.tensor_reduce(row_max[:, :], sumsq[:, :], AX.X, ALU.max).then_inc(row_max_ready, 1)
                dve.wait_ge(bank_filled[TOP_JOB[0]], use(TOP_JOB, b))
                nc.vector.tensor_reduce(top[:, 0:1], bank[TOP_JOB[0]][0:1, 0:TP], AX.X, ALU.max)\
                  .then_inc(bank_drained[TOP_JOB[0]], 1)
                dve.wait_ge(bank_drained[TOP_JOB[0]], use(TOP_JOB, b))
                nc.vector.tensor_scalar(scale_row[:, 2:3], top[:, 0:1], TINY, 2.0, ALU.max, ALU.mult).then_inc(scale_step, 1)
                dve.wait_ge(scale_step, 2 * b + 1)
                nc.vector.reciprocal(top[:, 1:2], scale_row[:, 2:3]).then_inc(scale_step, 1)
                dve.wait_ge(scale_step, 2 * b + 2)
                nc.vector.tensor_scalar(scale_row[:, 0:1], top[:, 1:2], 2.0 * GRAM_TOP, None, ALU.mult).then_inc(scale_row_ready, 1)
                nc.vector.tensor_scalar(scale_row[:, 1:2], top[:, 1:2], GRAM_TOP, None, ALU.mult).then_inc(scale_row_ready, 1)

                def residual(t):
                    j, c0, cn = (Q_JOB + K_JOB)[t], *CT[t % NC]
                    n = S if t < NC else T
                    dve.wait_ge(hi_split, 2 * NC * b + t + 1)
                    dve.wait_ge(parts_split, 2 * NC * b + t + 1)
                    nc.vector.scalar_tensor_tensor(resid[0:cn, t % R1, 0:n], bank[j[0]][0:cn, 0:n], 1.0 if t < NC else SCALE,
                                                   parts[0:cn, t, 0, 0:n], ALU.mult, ALU.subtract)\
                      .then_inc(bank_drained[j[0]], 1)

                for t in range(NC):
                    residual(t)
                dve.wait_ge(bank_filled[SCALE_JOB[0]], use(SCALE_JOB, b))
                nc.vector.tensor_copy(scale[:, b, :], bank[SCALE_JOB[0]][:, 0:3]).then_inc(bank_drained[SCALE_JOB[0]], 1)
                for t in range(NC, 2 * NC):
                    residual(t)
                for k in range(TT):
                    j = V_JOB[k]
                    v_k = v_sb[:, :, k, :]
                    dve.wait_ge(v_hi_split, TT * b + k + 1)
                    dve.wait_ge(v_split, TT * b + k + 1)
                    nc.vector.tensor_tensor(resid_v[:, k % RV, :].rearrange("p (h d) -> p h d", d=D),
                                            bank[j[0]][0:TP, 0:C].rearrange("p (h d) -> p h d", d=D), v_k[:, :, 0:D],
                                            ALU.subtract).then_inc(bank_drained[j[0]], 1)
                dve.wait_ge(bank_drained[SCALE_JOB[0]], use(SCALE_JOB, b))
                for k in range(TT):
                    j, n = G_JOB[k], U_COLS[k]
                    dve.wait_ge(u_hi_split, TT * b + k + 1)
                    if n > TP:
                        nc.vector.scalar_tensor_tensor(u_sb[:, 1, UL[k] + TP:UL[k] + n], bank[j[0]][0:TP, TP:n],
                                                       scale[0:TP, b, 0:1], u_sb[:, 1, UH[k] + TP:UH[k] + n],
                                                       ALU.mult, ALU.subtract)
                    nc.vector.scalar_tensor_tensor(u_sb[:, 1, UL[k]:UL[k] + TP], bank[j[0]][0:TP, 0:TP],
                                                   scale[0:TP, b, 1:2], u_sb[:, 1, UH[k]:UH[k] + TP],
                                                   ALU.mult, ALU.subtract).then_inc(bank_drained[j[0]], 1)

            def row_maximum(v, st):
                dve.wait_ge(scores_filled, v + 1)
                nc.vector.tensor_reduce(neg_max[:, st:st + 1], bank[S_BANK + st % 2][:, 0:T], AX.X, ALU.max, negate=True)\
                  .then_inc(row_max_found, 1)

            def norm(v, st):
                dve.wait_ge(quad_filled, v + 1)
                nc.vector.scalar_tensor_tensor(discard[:, st % 2, 0:T], bank[Y_BANK + st % 2][:, 0:T], 1.0, probs[:, st, :], ALU.mult,
                                               ALU.mult, accum_out=norms[:, bass.ds(v, 1)]).then_inc(norms_done, 1)

            def lo(v, par):
                dve.wait_ge(hi_ready, v + 1)
                nc.vector.scalar_tensor_tensor(probs_lo[:, par, :], bank[PT_BANK + par][0:TP, 0:S], PROB_SCALE,
                                               probs_hi[:, par, :], ALU.mult, ALU.subtract).then_inc(lo_ready, 1)

            def head_steps(g, first):
                for j in range(ST):
                    row_maximum(ST * g + j, j)
                    if not (first and j < 3):
                        norm(ST * g + j - 3, (j - 3) % ST)
                    if not (first and j == 0):
                        lo(ST * g + j - 1, (j - 1) % 2)

            head_steps(0, True)
            with dve.Fori(1, HEADS) as g:
                head_steps(g, False)
            norm(UNITS - 3, (UNITS - 3) % ST)
            lo(UNITS - 1, (UNITS - 1) % 2)
            norm(UNITS - 2, (UNITS - 2) % ST)
            norm(UNITS - 1, (UNITS - 1) % ST)

            dve.wait_ge(head_reduced, 2 + HEADS)
            dve.wait_ge(norms_done, 2 + UNITS)
            sums = reduced[:, :, :, RCOLS - 1]
            nc.vector.reciprocal(inv_sum.rearrange("p (g s) -> p g s", s=ST), sums).then_inc(inv_sum_ready, 1)
            nc.vector.scalar_tensor_tensor(square.rearrange("p (b u) -> p b u", b=B),
                                           norms[:, :].rearrange("p (b u) -> p b u", b=B), 0.0,
                                           scale[:, :, 2].unsqueeze(2).broadcast_to([P, B, H * ST]),
                                           ALU.max, ALU.mult).then_inc(square_ready, 1)
            dve.wait_ge(root_ready, 1)
            nc.vector.tensor_scalar(root2, root, 1e-18, None, ALU.max).then_inc(norm_step, 1)
            dve.wait_ge(norm_step, 1)
            nc.vector.reciprocal(inv_norm, root2).then_inc(norm_step, 1)
            dve.wait_ge(norm_step, 2)
            nc.vector.tensor_tensor(root, square, inv_norm, ALU.mult).then_inc(norm_step, 1)
            dve.wait_ge(norm_step, 3)
            nc.vector.tensor_tensor(square, root, root2, ALU.add).then_inc(norm_step, 1)
            dve.wait_ge(norm_step, 4)
            nc.vector.tensor_scalar(root2.rearrange("p (g s) -> p g s", s=ST), sums, EPS, None, ALU.mult).then_inc(norm_step, 1)
            dve.wait_ge(norm_step, 5)
            nc.vector.scalar_tensor_tensor(root, square, 0.5, root2, ALU.mult, ALU.max).then_inc(norm_step, 1)
            dve.wait_ge(norm_step, 6)
            nc.vector.reciprocal(inv_norm, root).then_inc(norm_step, 1)
            dve.wait_ge(norm_step, 7)
            dve.wait_ge(late_loaded, 16 * (1 + B))

            U = H * ST
            fused3 = fused.rearrange("p (u n) -> p u n", n=N_IP)
            exp3 = ip_exp.rearrange("p (u n) -> p u n", n=N_IP)
            stat, stat2 = ip_stat3[:, 0:U], ip_stat3[:, U:2 * U]

            def over_tokens(a):
                return a.unsqueeze(2).broadcast_to([P, U, N_IP])

            ELEM = 6

            def elem(b, par, free):
                step = ELEM * b
                red_b = reduced[:, bass.ds(b * H, H), :, D:D + N_IP].rearrange("p h s n -> p (h s) n")
                nc.vector.tensor_tensor(fused3, red_b, over_tokens(inv_norm[:, bass.ds(b * U, U)]), ALU.mult)\
                  .then_inc(elem_step, 1)
                dve.wait_ge(elem_step, step + 1)
                nc.vector.scalar_tensor_tensor(fused, ip_scores[:, b].rearrange("p h s n -> p (h s n)"), SCALE / SEM_SCALE,
                                               fused, ALU.mult, ALU.add).then_inc(elem_step, 1)
                dve.wait_ge(elem_step, step + 2)
                nc.vector.tensor_reduce(stat, fused3, AX.X, ALU.max).then_inc(elem_step, 1)
                dve.wait_ge(elem_step, step + 3)
                nc.vector.tensor_tensor(fused3, fused3, over_tokens(stat), ALU.subtract).then_inc(ip_fused, 1)
                dve.wait_ge(ip_exp_ready, b + 1)
                nc.vector.tensor_reduce(stat, exp3, AX.X, ALU.add).then_inc(elem_step, 1)
                dve.wait_ge(elem_step, step + 4)
                nc.vector.reciprocal(stat2, stat).then_inc(elem_step, 1)
                dve.wait_ge(elem_step, step + 5)
                nc.vector.tensor_tensor(stat.rearrange("p (h s) -> p h s", s=ST), stat2.rearrange("p (h s) -> p h s", s=ST),
                                        mask_col[:, :].unsqueeze(1).broadcast_to([P, H, ST]), ALU.mult).then_inc(elem_step, 1)
                dve.wait_ge(elem_step, step + 6)
                if free:
                    dve.wait_ge(text_t_filled, (NC + 1) * (b - 1))
                nc.vector.tensor_tensor(ip_probs[:, par].rearrange("p s (h n) -> p h s n", n=N_IP),
                                        exp3.rearrange("p (h s) n -> p h s n", s=ST),
                                        stat.rearrange("p (h s) -> p h s", s=ST).unsqueeze(3).broadcast_to([P, H, ST, N_IP]),
                                        ALU.mult).then_inc(ip_probs_ready, 1)

            def residual_add(b, half, par, free=True):
                dve.wait_ge(x_reloaded[par], 16 * (half + 1))
                for s in range(ST):
                    dve.wait_ge(y_filled, ST * b + s + 1)
                    if free:
                        dve.wait_ge(y_stored, 16 * ST * b)
                    nc.vector.tensor_tensor(y_sb[:, s, :], bank[4 + s][:, 0:C], x_sb[:, par, s, :], ALU.add)\
                      .then_inc(y_ready, 1)

            elem(0, 0, False)
            elem(1, 1, False)
            residual_add(0, 0, 0, False)
            with dve.Fori(1, B // 2) as pair:
                elem(2 * pair, 0, True)
                residual_add(2 * pair - 1, pair - 1, 1)
                elem(2 * pair + 1, 1, True)
                residual_add(2 * pair, pair, 0)
            residual_add(B - 1, B // 2 - 1, 1)

        @block.tensor
        def _(pe):
            pe.wait_ge(consts_made, CONSTS)
            pe.wait_ge(ip_loaded, 16 * B)
            for e in range(ET):
                last = nc.tensor.transpose(bank[0][:, e * ALLIP:(e + 1) * ALLIP], ip_rows[:, 0, e * P:(e + 1) * P],
                                           ident[0:ALLIP, 0:ALLIP])
            last.then_inc(bank_filled[0], 1)
            pe.wait_ge(ip_weights_loaded, 32)
            pe.wait_ge(bank_drained[0], 1)
            for j, w in ((2, wk_ip), (3, wv_ip)):
                for m, (c0, cn) in enumerate(CT):
                    for e in range(ET):
                        last = nc.tensor.matmul(bank[j][0:cn, m * ALLIP:(m + 1) * ALLIP], w[:, e, c0:c0 + cn], ip_t[:, e, :],
                                                start=(e == 0), stop=(e == ET - 1))
                last.then_inc(bank_filled[j], 1)
            pe.wait_ge(ip_step, 7)
            for e in range(ET):
                last = nc.tensor.transpose(bank[1][:, e * ALLIP:(e + 1) * ALLIP], ip_rows[:, 1, e * P:(e + 1) * P],
                                           ident[0:ALLIP, 0:ALLIP])
            last.then_inc(bank_filled[1], 1)
            pe.wait_ge(weights_loaded, 16 * 6)
            pe.wait_ge(bank_drained[3], 1)
            for b in range(B):
                pe.wait_ge(bank_drained[b], SETUP_USES[b] - 1)
                for c, (r0, rn) in enumerate(CT):
                    last = nc.tensor.matmul(bank[b][0:HIP, 0:C], vip_bd[0:rn, c, b, :], wout[0:rn, c, :],
                                            start=(c == 0), stop=(c == NC - 1))
                last.then_inc(bank_filled[b], 1)

            with pe.Fori(0, B) as b:
                def free(job):
                    pe.wait_ge(bank_drained[job[0]], use(job, b) - 1)

                pe.wait_ge(x_loaded, 16 * (b + 1))
                for j in XT_JOB:
                    free(j)
                for c, (c0, cn) in enumerate(CT):
                    j = XT_JOB[c]
                    for s in range(ST):
                        last = nc.tensor.transpose(bank[j[0]][0:cn, s * P:(s + 1) * P], x_sb[:, 0, s, c0:c0 + cn], ident[:, :])
                    last.then_inc(bank_filled[j[0]], 1)
                pe.wait_ge(ctx_loaded, 16 * (b + 1))
                for e in range(ET):
                    j = CT_JOB[e]
                    free(j)
                    for k in range(TT):
                        last = nc.tensor.transpose(bank[j[0]][:, k * TP:(k + 1) * TP], ctx_sb[:, k, e * P:(e + 1) * P],
                                                   ident[0:TP, 0:TP])
                    last.then_inc(bank_filled[j[0]], 1)
                free(TOP_JOB)
                pe.wait_ge(row_max_ready, b + 1)
                nc.tensor.transpose(bank[TOP_JOB[0]][0:1, 0:TP], row_max[:, :], ident[0:TP, 0:TP])\
                  .then_inc(bank_filled[TOP_JOB[0]], 1)
                for m, (c0, cn) in enumerate(CT):
                    j = Q_JOB[m]
                    pe.wait_ge(bank_drained[XT_JOB[-1][0]], use(XT_JOB[-1], b))
                    free(j)
                    for c, (r0, rn) in enumerate(CT):
                        last = nc.tensor.matmul(bank[j[0]][0:cn, 0:S], wq[0:rn, c, c0:c0 + cn], x_t[0:rn, c, :],
                                                start=(c == 0), stop=(c == NC - 1))
                    last.then_inc(bank_filled[j[0]], 1)
                free(SCALE_JOB)
                pe.wait_ge(scale_row_ready, 2 * (b + 1))
                nc.tensor.matmul(bank[SCALE_JOB[0]][:, 0:3], ones_row[:, :], scale_row[:, :], start=True, stop=True)\
                  .then_inc(bank_filled[SCALE_JOB[0]], 1)
                pe.wait_ge(bank_drained[CT_JOB[-1][0]], use(CT_JOB[-1], b))
                for m, (c0, cn) in enumerate(CT):
                    j = K_JOB[m]
                    free(j)
                    for e in range(ET):
                        last = nc.tensor.matmul(bank[j[0]][0:cn, 0:T], wk[:, e, c0:c0 + cn], ctx_t[:, e, :],
                                                start=(e == 0), stop=(e == ET - 1))
                    last.then_inc(bank_filled[j[0]], 1)
                pe.wait_ge(bank_drained[1], 1)
                for k in range(TT):
                    j = V_JOB[k]
                    free(j)
                    for e in range(ET):
                        last = nc.tensor.matmul(bank[j[0]][0:TP, 0:C + ALLIP], ctx_t[:, e, k * TP:(k + 1) * TP], wvx[:, e, :],
                                                start=(e == 0), stop=(e == ET - 1))
                    last.then_inc(bank_filled[j[0]], 1)
                free(IPS_JOB)
                pe.wait_ge(q_full_ready, NC * (b + 1))
                pe.wait_ge(bank_drained[2], 1)
                for s in range(ST):
                    for c, (r0, rn) in enumerate(CT):
                        last = nc.tensor.matmul(bank[IPS_JOB[0]][:, s * HIP:(s + 1) * HIP], q_full[0:rn, c, s * P:(s + 1) * P],
                                                kip_bd[0:rn, c, b, :], start=(c == 0), stop=(c == NC - 1))
                last.then_inc(bank_filled[IPS_JOB[0]], 1)
                for k in range(TT):
                    j = G_JOB[k]
                    free(j)
                    for e in range(ET):
                        last = nc.tensor.matmul(bank[j[0]][0:TP, 0:U_COLS[k]], ctx_t[:, e, k * TP:(k + 1) * TP],
                                                ctx_t[:, e, k * TP:T], start=(e == 0), stop=(e == ET - 1))
                    last.then_inc(bank_filled[j[0]], 1)

            for j in range(8):
                pe.wait_ge(bank_drained[j], end_of_phase1(j))

            def scores(r, st, blk, u, free):
                if st == 0:
                    pe.wait_ge(head_loaded[r], 16 * 10 * (blk + 1))
                if free:
                    pe.wait_ge(probs_ready, u - 1)
                nc.tensor.matmul(bank[S_BANK + st % 2][:, 0:T], q_ring[:, r, st * P:(st + 1) * P], k_ring[:, r, :],
                                 start=True, stop=True).then_inc(scores_filled, 1)

            def transposes(st, u):
                pe.wait_ge(probs_ready, u + 1)
                for k in range(TT):
                    last = nc.tensor.transpose(bank[PT_BANK + st % 2][0:TP, k * P:(k + 1) * P],
                                               probs[:, st, k * TP:(k + 1) * TP], ident[:, :])
                last.then_inc(probs_t_filled, 1)

            def unit(j, u, blk, par, ahead):
                r, st = j // ST, j % ST
                y, o = bank[Y_BANK + st % 2][:, 0:T], bank[O_BANK + st // 2][:, (st % 2) * VCOLS:(st % 2 + 1) * VCOLS]

                if ahead > 1:
                    scores((j + 2) // ST % RING, (st + 2) % ST, blk + (j + 2) // BLK, u + 2, True)
                pe.wait_ge(hi_ready, u + 1)
                pe.wait_ge(norms_done, u + 1)
                if st % 2 == 0:
                    pe.wait_ge(out_drained, BLK // 2 * blk + j // 2 + 1)
                for k in range(TT):
                    hi_k = probs_hi[:, st % 2, k * P:(k + 1) * P]
                    nc.tensor.matmul(y[:, k * TP:T], hi_k, u_sb[:, par, UH[k]:UH[k] + U_COLS[k]], start=(k == 0), stop=False)
                    nc.tensor.matmul(y[:, k * TP:T], hi_k, u_sb[:, par, UL[k]:UL[k] + U_COLS[k]], start=False, stop=False)
                    nc.tensor.matmul(o, hi_k, v_ring[:, r, k, :], start=(k == 0), stop=False)
                if ahead > 0:
                    transposes((st + 1) % ST, u + 1)
                pe.wait_ge(lo_ready, u + 1)
                for k in range(TT):
                    lo_k = probs_lo[:, st % 2, k * P:(k + 1) * P]
                    last_o = nc.tensor.matmul(o, lo_k, v_ring[:, r, k, :], start=False, stop=(k == TT - 1))
                    last_y = nc.tensor.matmul(y[:, k * TP:T], lo_k, u_sb[:, par, UH[k]:UH[k] + U_COLS[k]], start=False,
                                              stop=(k == TT - 1))
                    if k == TT - 1 and st % 2 == 1:
                        last_o.then_inc(out_filled, 1)
                last_y.then_inc(quad_filled, 1)

            def heads(blk, par, last):
                for j in range(BLK):
                    unit(j, BLK * blk + j, blk, par, BLK - 1 - j if last else 2)

            scores(0, 0, 0, 0, False)
            scores(0, 1, 0, 1, False)
            transposes(0, 0)
            with pe.Fori(0, B // 2 - 1) as pair:
                for par in range(2):
                    pe.wait_ge(u_loaded, 16 * (2 * pair + par + 1))
                    apart(pe)
                    with pe.Fori(0, BLOCKS) as i:
                        heads(BLOCKS * (2 * pair + par) + i, par, False)
            pe.wait_ge(u_loaded, 16 * (B - 1))
            with pe.Fori(0, BLOCKS) as i:
                heads(BLOCKS * (B - 2) + i, 0, False)
            pe.wait_ge(u_loaded, 16 * B)
            with pe.Fori(0, BLOCKS - 1) as i:
                heads(BLOCKS * (B - 1) + i, 1, False)
            heads(BLOCKS * B - 1, 1, True)

            pe.wait_ge(norms_done, 2 + UNITS)
            pe.wait_ge(out_drained, 2 + 2 * HEADS)

            def text_transposes(b, par, free):
                pe.wait_ge(text_ready, b + 1)
                if free:
                    pe.wait_ge(text_t_ready, (NC + 1) * b)
                for c, (c0, cn) in enumerate(CT):
                    for s in range(ST):
                        last = nc.tensor.transpose(bank[c][0:cn, s * P:(s + 1) * P], text[:, par, s, c0:c0 + cn], ident[:, :])
                    last.then_inc(text_t_filled, 1)
                pe.wait_ge(ip_probs_ready, b + 1)
                for s in range(ST):
                    last = nc.tensor.transpose(bank[NC][0:HIP, s * P:(s + 1) * P], ip_probs[:, par, s, :], ident[:, :])
                last.then_inc(text_t_filled, 1)

            def project(b, par, free):
                pe.wait_ge(text_t_ready, (NC + 1) * (b + 1))
                for s in range(ST):
                    if free:
                        pe.wait_ge(y_ready, ST * (b - 1) + s + 1)
                    y = bank[4 + s][:, 0:C]
                    for c, (c0, cn) in enumerate(CT):
                        nc.tensor.matmul(y, text_t[0:cn, par, c, s * P:(s + 1) * P], wout[0:cn, c, :], start=(c == 0), stop=False)
                    nc.tensor.matmul(y, ip_probs_t[0:HIP + 1, par, s * P:(s + 1) * P], vw[0:HIP + 1, b, :], start=False,
                                     stop=True).then_inc(y_filled, 1)

            pe.wait_ge(late_loaded, 16 * (1 + B))
            text_transposes(0, 0, False)
            text_transposes(1, 1, True)
            project(0, 0, False)
            with pe.Fori(1, B // 2) as pair:
                text_transposes(2 * pair, 0, True)
                project(2 * pair - 1, 1, True)
                text_transposes(2 * pair + 1, 1, True)
                project(2 * pair, 0, True)
            project(B - 1, 1, True)


INPUTS = ["x", "ctx_2048", "fside_S_0", "L0_xattn_W_q", "L0_xattn_W_k", "L0_xattn_W_v", "L0_xattn_W_k_ip",
          "L0_xattn_W_v_ip", "L0_xattn_W_out", "L0_xattn_b_out"]


def kernel(**inputs):
    import numpy as np
    import concourse.bacc as bacc
    from concourse import mybir
    from concourse.bass_utils import run_bass_kernel_spmd

    nc = bacc.Bacc("TRN2", target_bir_lowering=False, num_devices=1)
    arrays, args = {}, []
    for name in INPUTS:
        a = np.ascontiguousarray(inputs[name])
        arrays[f"in_{name}"] = a
        args.append(nc.dram_tensor(f"in_{name}", a.shape, mybir.dt.from_np(a.dtype), kind="ExternalInput").ap())
    args.append(nc.dram_tensor("result", inputs["x"].shape, mybir.dt.float32, kind="ExternalOutput").ap())
    xattn_kernel(nc, *args)
    r = run_bass_kernel_spmd(nc, [arrays], core_ids=[0])
    return r.results[0]["result"]
```

```python
import concourse.bass as bass
from concourse import mybir
from contextlib import ExitStack


def xattn_kernel(
    nc: bass.Bass,
    x: bass.AP,
    ctx: bass.AP,
    spatial_mask: bass.AP,
    w_q: bass.AP,
    w_k: bass.AP,
    w_v: bass.AP,
    w_k_ip: bass.AP,
    w_v_ip: bass.AP,
    w_out: bass.AP,
    b_out: bass.AP,
    out: bass.AP,
):
    fp32 = mybir.dt.float32
    fp16 = mybir.dt.float16
    bf16 = mybir.dt.bfloat16
    ALU = mybir.AluOpType
    ACT = mybir.ActivationFunctionType
    AX = mybir.AxisListType

    B, S, C = x.shape
    E = ctx.shape[2]
    N_IP = 4
    T = ctx.shape[1] - N_IP
    H = 20
    D = C // H
    SCALE = float(D) ** -0.5
    SEM_SCALE = 0.5
    EPS = 1e-12
    TINY = 1e-30
    P = 128
    ST = S // P
    TT = 4
    TP = T // TT
    ET = E // P
    CT = [(c, min(P, C - c)) for c in range(0, C, P)]
    NC = len(CT)
    HIP = H * N_IP
    ALLIP = B * N_IP
    PROB_SCALE = 2.0 ** 14
    GRAM_TOP = 2.0 ** 14
    VW_PART = D + N_IP
    VCOLS = 3 * VW_PART + 1
    RCOLS = VW_PART + 1
    U_COLS = [T - TP * k for k in range(TT)]
    GH = [T * k for k in range(TT)]
    UL = [T * TT + sum(U_COLS[:k]) for k in range(TT)]
    U_ALL = T * TT + sum(U_COLS)
    PAIRS = [(0, 0), (1, 0), (2, 0), (0, 1), (1, 1), (0, 2)]
    KS = len(PAIRS) * D
    HEADS = B * H
    UNITS = HEADS * ST
    RING = 4
    BLK = RING * ST
    BLOCKS = H // RING

    q_parts = nc.dram_tensor("q_parts", [B, 3, C, S], bf16).ap()
    k_parts = nc.dram_tensor("k_parts", [B, 3, C, T], bf16).ap()
    v_parts = nc.dram_tensor("v_parts", [B, H, TP, TT * VCOLS], bf16).ap()
    u_parts = nc.dram_tensor("u_parts", [B, TP, U_ALL], fp16).ap()

    stack = ExitStack()
    with stack:
        def sb(name, shape, dt):
            return stack.enter_context(nc.sbuf_tensor(name, shape, dt))

        def sem(name):
            return stack.enter_context(nc.semaphore(name))

        ident = sb("ident", [P, P], fp32)
        ident16 = sb("ident16", [P, P], fp16)
        ones_row = sb("ones_row", [1, P], fp32)
        headmask = sb("headmask", [P, NC, H], fp32)
        mask_col = sb("mask_col", [P, ST], fp32)
        wq = sb("wq", [P, NC, C], fp32)
        wk = sb("wk", [P, ET, C], fp32)
        wvx = sb("wvx", [P, ET, C + ALLIP], fp32)
        wout = sb("wout", [P, NC, C], fp32)
        kip_bd = sb("kip_bd", [P, NC, B, HIP], fp32)
        ip_scores = sb("ip_scores", [P, B, H, ST, N_IP], fp32)
        vw = sb("vw", [96, B, C], fp32)
        scale = sb("scale", [P, B, 3], fp32)
        reduced = sb("reduced", [P, HEADS, ST, RCOLS], fp32)
        norms = sb("norms", [P, UNITS], fp32)
        x_sb = sb("x_sb", [P, 2, ST, C], fp32)
        u_sb = sb("u_sb", [TP, 2, U_ALL], fp16)
        v_ring = sb("v_ring", [TP, RING, TT, VCOLS], bf16)
        q_ring = sb("q_ring", [KS, RING, S], bf16)
        k_ring = sb("k_ring", [KS, RING, T], bf16)
        probs = sb("probs", [P, ST, T], fp32)
        half_hi = sb("half_hi", [P, 2, T], fp16)
        weight = sb("weight", [P, 2, T], fp32)
        neg_max = sb("neg_max", [P, ST], fp32)
        probs_hi = sb("probs_hi", [TP, 2, S], fp16)
        probs_lo = sb("probs_lo", [TP, 2, S], fp16)
        discard = sb("discard", [P, 2, E], fp32)
        out_raw = sb("out_raw", [P, 4, 2, VCOLS], fp32)
        v_sb = sb("v_sb", [TP, H, TT, VCOLS], bf16)
        work = sb("work", [P, 2 * NC * S], fp32)
        late = sb("late", [P, 2 * NC * 3 * S // 2], fp32)
        parts = late[:, :].bitcast(bf16).rearrange("p (t a s) -> p t a s", t=2 * NC, a=3)
        q_full = work[:, 0:NC * S].rearrange("p (c s) -> p c s", c=NC)
        resid = work[:, NC * S:2 * NC * S].rearrange("p (r s) -> p r s", r=3)
        resid_v = sb("resid_v", [TP, 2, C], fp32)
        sem_raw = sb("sem_raw", [TP, TT, N_IP], fp32)
        sem_res = sb("sem_res", [TP, 2, TT, N_IP], fp32)
        gram_hi2 = sb("gram_hi2", [TP, 2, T - TP], fp16)
        sumsq = sb("sumsq", [TP, TT], fp32)
        row_max = sb("row_max", [TP, 1], fp32)
        top = sb("top", [1, 2], fp32)
        scale_row = sb("scale_row", [1, 3], fp32)
        ip_stat = sb("ip_stat", [ALLIP, 8], fp32)
        spare = reduced[:, :, :, :].rearrange("p g s c -> p (g s c)")
        taken = [0]

        def carve(parts_n, n):
            a = spare[0:parts_n, taken[0]:taken[0] + n]
            taken[0] += n
            assert taken[0] <= HEADS * ST * RCOLS
            return a

        ctx_sb = carve(TP, TT * E).rearrange("p (k e) -> p k e", k=TT)
        ctx_t = carve(P, ET * T).rearrange("p (e t) -> p e t", e=ET)
        x_t = carve(P, NC * S).rearrange("p (c s) -> p c s", c=NC)
        wk_ip = carve(P, ET * C).rearrange("p (e c) -> p e c", e=ET)
        wv_ip = carve(P, ET * C).rearrange("p (e c) -> p e c", e=ET)
        vip_bd = carve(P, NC * B * HIP).rearrange("p (m b c) -> p m b c", m=NC, b=B)
        ip_rows = carve(ALLIP, 2 * E).rearrange("p (a e) -> p a e", a=2)
        ip_t = carve(P, ET * ALLIP).rearrange("p (e i) -> p e i", e=ET)
        NS, U = 2 * ST * C, H * ST
        text = late[:, 0:NS].rearrange("p (a s c) -> p a s c", a=2, s=ST)
        square, root = (late[:, NS + n * UNITS:NS + (n + 1) * UNITS] for n in range(2))
        inv_sum = late[:, NS + 2 * UNITS:NS + 2 * UNITS + 2 * U].rearrange("p (a u) -> p a u", a=2)
        text_t = work[:, :].rearrange("p (a c s) -> p a c s", a=2, c=NC)
        over_probs = probs[:, :, :].rearrange("p s t -> p (s t)")
        fused, ip_exp = (over_probs[:, n * ST * HIP:(n + 1) * ST * HIP] for n in range(2))
        norm_tmp = [over_probs[:, 2 * ST * HIP + n * U:2 * ST * HIP + (n + 1) * U] for n in range(7)]
        ip_stat3 = sb("ip_stat3", [P, 2 * ST * H], fp32)
        ip_probs_t = sb("ip_probs_t", [96, 2, S], fp32)
        over_kip = kip_bd[:, :, :, :].rearrange("p m b c -> p (m b c)")
        y_sb = over_kip[:, 0:ST * C].rearrange("p (s c) -> p s c", s=ST)
        ip_probs = over_kip[:, ST * C:ST * C + 2 * ST * HIP].rearrange("p (a s c) -> p a s c", a=2, s=ST)

        bank = [stack.enter_context(nc.psum_tensor(f"bank{j}", [P, 512], fp32)) for j in range(8)]
        def bank16(j):
            return bank[j][:, :].bitcast(fp16)

        GT_COL = [0, 0, P, 3 * P]
        S_BANK, PT_BANK, Y_BANK, O_BANK = 0, 2, 4, 6

        consts_made = sem("consts_made")
        unwatched = sem("unwatched")
        ip_loaded = sem("ip_loaded")
        ip_weights_loaded = sem("ip_weights_loaded")
        weights_loaded = sem("weights_loaded")
        late_loaded = sem("late_loaded")
        ip_step = sem("ip_step")
        ip_root = sem("ip_root")
        bank_filled = [sem(f"bank_filled{j}") for j in range(8)]
        bank_drained = [sem(f"bank_drained{j}") for j in range(8)]
        x_loaded = sem("x_loaded")
        ctx_loaded = sem("ctx_loaded")
        x_reloaded = [sem(f"x_reloaded{par}") for par in range(2)]
        x_t_ready = sem("x_t_ready")
        ctx_t_ready = sem("ctx_t_ready")
        scale_step = sem("scale_step")
        sumsq_ready = sem("sumsq_ready")
        row_max_ready = sem("row_max_ready")
        scale_row_ready = sem("scale_row_ready")
        q_full_ready = sem("q_full_ready")
        hi_split = sem("hi_split")
        mid_split = sem("mid_split")
        parts_split = sem("parts_split")
        parts_saved = sem("parts_saved")
        v_hi_split = sem("v_hi_split")
        v_mid_split = sem("v_mid_split")
        v_split = sem("v_split")
        sem_step = sem("sem_step")
        gram_hi_split = sem("gram_hi_split")
        gram_hi2_split = sem("gram_hi2_split")
        v_saved = sem("v_saved")
        u_saved = sem("u_saved")
        head_loaded = [sem(f"head_loaded{r}") for r in range(RING)]
        u_loaded = sem("u_loaded")
        scores_filled = sem("scores_filled")
        row_max_found = sem("row_max_found")
        probs_ready = sem("probs_ready")
        probs_t_filled = sem("probs_t_filled")
        hi_ready = sem("hi_ready")
        lo_ready = sem("lo_ready")
        quad_filled = sem("quad_filled")
        half_ready = sem("half_ready")
        weight_ready = sem("weight_ready")
        norms_done = sem("norms_done")
        out_filled = sem("out_filled")
        out_drained = sem("out_drained")
        pool_sum = sem("pool_sum")
        head_reduced = sem("head_reduced")
        norm_step = sem("norm_step")
        square_ready = sem("square_ready")
        root_ready = sem("root_ready")
        inv_sum_ready = sem("inv_sum_ready")
        elem_step = sem("elem_step")
        ip_fused = sem("ip_fused")
        ip_exp_ready = sem("ip_exp_ready")
        ip_probs_ready = sem("ip_probs_ready")
        text_ready = sem("text_ready")
        text_t_filled = sem("text_t_filled")
        text_t_ready = sem("text_t_ready")
        y_filled = sem("y_filled")
        y_ready = sem("y_ready")
        y_stored = sem("y_stored")

        SETUP_USES = [2, 2, 2, 2, 1, 1, 1, 1]
        USES = [3, 3, 3, 3, 3, 3, 3, 4]
        R1 = 3
        RV = 2
        Q_JOB = [(0, 2), (1, 2), (2, 2)]
        XT_JOB = [(0, 1), (1, 1), (2, 1)]
        CT_JOB = [(3, 1), (4, 1), (5, 1), (6, 1)]
        TOP_JOB, SCALE_JOB = (7, 1), (7, 2)
        K_JOB = [(3, 2), (4, 2), (5, 2)]
        V_JOB = [(6, 2), (7, 3), (0, 3), (1, 3)]
        IPS_JOB = (2, 3)
        G_JOB, GT_JOB = [(4, 3), (5, 3), (6, 3), (7, 4)], (3, 3)

        def use(job, b):
            return SETUP_USES[job[0]] + USES[job[0]] * b + job[1]

        def end_of_phase1(j):
            return SETUP_USES[j] + USES[j] * B

        CONSTS = 10

        def apart(eng):
            eng.sem_inc(unwatched, 1)

        block = stack.enter_context(nc.Block())

        @block.sync
        def _(sp):
            for b in range(B):
                sp.dma_start(ip_rows[b * N_IP:(b + 1) * N_IP, 0, :], ctx[b, T:T + N_IP, :]).then_inc(ip_loaded, 16)
            ctx_in = ctx[:, 0:T, :].rearrange("b (k p) e -> b p k e", p=TP)
            x_in = x.rearrange("b (s p) c -> b p s c", p=P)
            sp.dma_start(x_sb[:, 0], x_in[0]).then_inc(x_loaded, 16)
            sp.dma_start(ctx_sb, ctx_in[0]).then_inc(ctx_loaded, 16)
            sp.dma_start(wk_ip, w_k_ip.rearrange("(e p) c -> p e c", p=P)).then_inc(ip_weights_loaded, 16)
            sp.dma_start(wv_ip, w_v_ip.rearrange("(e p) c -> p e c", p=P)).then_inc(ip_weights_loaded, 16)

            def store_batch(b):
                for t in range(2 * NC):
                    c0, cn = CT[t % NC]
                    sp.wait_ge(parts_split, R1 + 2 * NC * b + t + 1)
                    dst = (q_parts if t < NC else k_parts)[b, :, c0:c0 + cn, :].rearrange("a c s -> c a s")
                    n = S if t < NC else T
                    sp.dma_start(dst, parts[0:cn, t, :, 0:n]).then_inc(parts_saved, 16)
                sp.wait_ge(v_split, RV + TT * (b + 1))
                apart(sp)
                sp.wait_ge(sem_step, 5 * (b + 1))
                sp.dma_start(v_parts[b].rearrange("h p c -> p h c"), v_sb[:, :, :, :].rearrange("p h k c -> p h (k c)"))\
                  .then_inc(v_saved, 16)
                sp.wait_ge(bank_drained[GT_JOB[0]], use(GT_JOB, b))
                sp.wait_ge(bank_drained[G_JOB[-1][0]], use(G_JOB[-1], b))
                sp.dma_start(u_parts[b], u_sb[:, 1, :]).then_inc(u_saved, 16)

            with sp.Fori(0, B - 1) as b:
                sp.wait_ge(bank_filled[XT_JOB[-1][0]], use(XT_JOB[-1], b))
                sp.dma_start(x_sb[:, 0], x_in[b + 1]).then_inc(x_loaded, 16)
                sp.wait_ge(bank_filled[CT_JOB[-1][0]], use(CT_JOB[-1], b))
                sp.wait_ge(row_max_ready, b + 1)
                sp.dma_start(ctx_sb, ctx_in[b + 1]).then_inc(ctx_loaded, 16)
                store_batch(b)

            def load_u(b, par):
                sp.dma_start(u_sb[:, par, :], u_parts[b]).then_inc(u_loaded, 16)

            def load_heads(b, i, blk, free):
                for r in range(RING):
                    rows = bass.ds(i * (RING * D) + r * D, D)
                    if free:
                        sp.wait_ge(scores_filled, BLK * blk + ST * (r + 1) - BLK)
                    for a0, n in ((0, 3), (3, 2), (5, 1)):
                        sp.dma_start(q_ring[a0 * D:(a0 + n) * D, r, :], q_parts[b, 0:n, rows, :])\
                          .then_inc(head_loaded[r], 16)
                    if free:
                        sp.wait_ge(out_filled, BLK // 2 * blk + ST // 2 * (r + 1) - BLK // 2)
                    sp.dma_start(v_ring[:, r].rearrange("p k c -> p (k c)"), v_parts[b, bass.ds(i * RING + r, 1), :, :]
                                 .rearrange("a p c -> p (a c)")).then_inc(head_loaded[r], 16)
                    for a, (_, kp) in enumerate(PAIRS):
                        sp.dma_start(k_ring[a * D:(a + 1) * D, r, :], k_parts[b, kp, rows, :])\
                          .then_inc(head_loaded[r], 16)

            sp.wait_ge(u_saved, 1 + 16)
            load_u(0, 0)
            sp.wait_ge(parts_saved, 1 + 16 * 2 * NC)
            sp.wait_ge(v_saved, 1 + 16)
            load_heads(0, 0, 0, False)
            store_batch(B - 1)
            sp.wait_ge(parts_saved, 1 + 16 * 2 * NC * B)
            sp.wait_ge(v_saved, 1 + 16 * B)
            sp.wait_ge(u_saved, 1 + 16 * B)
            with sp.Fori(1, BLOCKS) as i:
                load_heads(0, i, i, True)
            load_u(1, 1)
            with sp.Fori(0, BLOCKS) as i:
                load_heads(1, i, BLOCKS + i, True)
            with sp.Fori(1, B // 2) as pair:
                for par in range(2):
                    sp.wait_ge(quad_filled, H * ST * (2 * pair + par - 1))
                    apart(sp)
                    load_u(2 * pair + par, par)
                    with sp.Fori(0, BLOCKS) as i:
                        load_heads(2 * pair + par, i, BLOCKS * (2 * pair + par) + i, True)

            def load_x(b, par):
                sp.dma_start(x_sb[:, par], x_in[b]).then_inc(x_reloaded[par], 16)

            out_v = out.rearrange("b (s p) c -> b p s c", p=P)

            def store_y(b):
                for s in range(ST):
                    sp.wait_ge(y_ready, ST * b + s + 1)
                    sp.dma_start(out_v[b, :, s, :], y_sb[:, s, :]).then_inc(y_stored, 16)

            sp.wait_ge(bank_filled[XT_JOB[-1][0]], use(XT_JOB[-1], B - 1))
            load_x(0, 0)
            load_x(1, 1)
            with sp.Fori(0, B // 2 - 1) as pair:
                for par in range(2):
                    store_y(2 * pair + par)
                    load_x(2 * pair + par + 2, par)
            store_y(B - 2)
            store_y(B - 1)
            sp.wait_ge(y_stored, 16 * ST * B)

        @block.gpsimd
        def _(pool):
            nc.gpsimd.memset(ident[:, :], 0.0).then_inc(consts_made, 1)
            nc.gpsimd.memset(ident16[:, :], 0.0).then_inc(consts_made, 1)
            nc.gpsimd.memset(headmask[:, :, :], 1.0).then_inc(consts_made, 1)
            nc.gpsimd.memset(ones_row[:, :], 1.0).then_inc(consts_made, 1)
            nc.gpsimd.memset(ip_probs_t[:, :, :], 1.0).then_inc(consts_made, 1)
            nc.gpsimd.memset(v_sb[:, :, :, VCOLS - 1:VCOLS], 1.0).then_inc(consts_made, 1)
            pool.wait_ge(consts_made, 6)
            nc.gpsimd.affine_select(out=ident[:, :], in_=ident[:, :], compare_op=ALU.not_equal, fill=1.0, base=0,
                                    pattern=[[-1, P]], channel_multiplier=1).then_inc(consts_made, 1)
            nc.gpsimd.affine_select(out=ident16[:, :], in_=ident16[:, :], compare_op=ALU.not_equal, fill=1.0, base=0,
                                    pattern=[[-1, P]], channel_multiplier=1).then_inc(consts_made, 1)
            nc.gpsimd.affine_select(out=headmask[:, :, :], in_=headmask[:, :, :], compare_op=ALU.is_ge, fill=0.0,
                                    base=0, pattern=[[P, NC], [-D, H]], channel_multiplier=1).then_inc(consts_made, 1)
            pool.wait_ge(consts_made, 9)
            nc.gpsimd.affine_select(out=headmask[:, :, :], in_=headmask[:, :, :], compare_op=ALU.is_ge, fill=0.0,
                                    base=D - 1, pattern=[[-P, NC], [D, H]], channel_multiplier=-1)\
              .then_inc(consts_made, 1)
            pool.sem_inc(parts_split, R1)
            pool.sem_inc(v_split, RV)
            pool.sem_inc(head_reduced, 2)
            pool.sem_inc(weight_ready, 2)
            for saved in (parts_saved, v_saved, u_saved):
                pool.sem_inc(saved, 1)

            with pool.Fori(0, B) as b:
                for t in range(2 * NC):
                    j, c0, cn = (Q_JOB + K_JOB)[t], *CT[t % NC]
                    n = S if t < NC else T
                    pool.wait_ge(bank_drained[j[0]], use(j, b))
                    apart(pool)
                    nc.gpsimd.tensor_copy(parts[0:cn, t, 1, 0:n], resid[0:cn, t % R1, 0:n]).then_inc(mid_split, 1)
                    pool.wait_ge(mid_split, 2 * NC * b + t + 1)
                    nc.gpsimd.tensor_tensor(parts[0:cn, t, 2, 0:n], resid[0:cn, t % R1, 0:n], parts[0:cn, t, 1, 0:n],
                                            ALU.subtract).then_inc(parts_split, 1)
                for k in range(TT):
                    j = V_JOB[k]
                    v_k = v_sb[:, :, k, :]
                    r_k = resid_v[:, k % RV, :].rearrange("p (h d) -> p h d", d=D)
                    pool.wait_ge(bank_drained[j[0]], use(j, b))
                    apart(pool)
                    nc.gpsimd.tensor_copy(v_k[:, :, VW_PART:VW_PART + D], r_k).then_inc(v_mid_split, 1)
                    pool.wait_ge(v_mid_split, TT * b + k + 1)
                    nc.gpsimd.tensor_tensor(v_k[:, :, 2 * VW_PART:2 * VW_PART + D], r_k,
                                            v_k[:, :, VW_PART:VW_PART + D], ALU.subtract).then_inc(v_split, 1)
                pool.wait_ge(v_hi_split, TT * (b + 1))
                apart(pool)

                def sem_part(a):
                    return v_sb[:, :, :, a * VW_PART + D:(a + 1) * VW_PART]

                def to_heads(src):
                    return src.unsqueeze(1).broadcast_to([TP, H, TT, N_IP])

                src = sem_raw[:, :, :]
                for a in range(3):
                    nc.gpsimd.tensor_copy(sem_part(a), to_heads(src)).then_inc(sem_step, 1)
                    if a < 2:
                        pool.wait_ge(sem_step, 5 * b + 2 * a + 1)
                        nc.gpsimd.tensor_tensor(sem_res[:, a], src, sem_part(a)[:, 0, :, :],
                                                ALU.subtract).then_inc(sem_step, 1)
                        pool.wait_ge(sem_step, 5 * b + 2 * a + 2)
                        apart(pool)
                        src = sem_res[:, a]

            def weigh(v, st):
                pool.wait_ge(half_ready, v + 1)
                pool.wait_ge(norms_done, v + 1)
                nc.gpsimd.tensor_tensor(weight[:, st % 2, :], probs[:, st, :], half_hi[:, st % 2, :], ALU.subtract)\
                  .then_inc(weight_ready, 1)

            def reduce_head(g, slot):
                pool.wait_ge(out_drained, 2 + 2 * g + 2)
                apart(pool)
                raw = out_raw[:, 2 * slot:2 * slot + 2].rearrange("p a u c -> p (a u) c")
                nc.gpsimd.tensor_tensor(reduced[:, g, :, 0:VW_PART], raw[:, :, 0:VW_PART],
                                        raw[:, :, VW_PART:2 * VW_PART], ALU.add).then_inc(pool_sum, 1)
                nc.gpsimd.tensor_copy(reduced[:, g, :, VW_PART:RCOLS], raw[:, :, VCOLS - 1:VCOLS])
                pool.wait_ge(pool_sum, g + 1)
                apart(pool)
                nc.gpsimd.tensor_tensor(reduced[:, g, :, 0:VW_PART], reduced[:, g, :, 0:VW_PART],
                                        raw[:, :, 2 * VW_PART:3 * VW_PART], ALU.add).then_inc(head_reduced, 1)

            def head_steps(g, slot, first):
                for j in range(ST):
                    weigh(ST * g + j, j)
                    if j == ST - 1 and not first:
                        reduce_head(g - 1, (slot - 1) % 2)

            head_steps(0, 0, True)
            head_steps(1, 1, False)
            with pool.Fori(1, HEADS // 2) as g2:
                for slot in range(2):
                    head_steps(2 * g2 + slot, slot, False)
            reduce_head(HEADS - 1, 1)

            pool.wait_ge(head_reduced, 2 + HEADS)

            def step(b, par, free):
                if free:
                    pool.wait_ge(text_t_filled, (NC + 1) * (b - 1))
                    apart(pool)
                    apart(pool)
                pool.wait_ge(inv_sum_ready, b + 1)
                apart(pool)
                red_b = reduced[:, bass.ds(b * H, H), :, 0:D]
                inv_b = inv_sum[:, par, :].rearrange("p (h s) -> p h s", s=ST)
                nc.gpsimd.tensor_tensor(text[:, par].rearrange("p s (h d) -> p h s d", d=D), red_b,
                                        inv_b.unsqueeze(3).broadcast_to([P, H, ST, D]), ALU.mult)\
                  .then_inc(text_ready, 1)

            step(0, 0, False)
            step(1, 1, False)
            with pool.Fori(1, B // 2) as pair:
                for par in range(2):
                    step(2 * pair + par, par, True)

        @block.scalar
        def _(act):
            act.dma_start(wq[:, 0:2, :], w_q[0:2 * P, :].rearrange("(m p) c -> p m c", p=P)).then_inc(weights_loaded, 16)
            act.dma_start(wq[0:CT[2][1], 2, :], w_q[2 * P:C, :]).then_inc(weights_loaded, 16)
            act.dma_start(wk[:, :, :], w_k.rearrange("(e p) c -> p e c", p=P)).then_inc(weights_loaded, 16)
            act.dma_start(wvx[:, :, 0:C], w_v.rearrange("(e p) c -> p e c", p=P)).then_inc(weights_loaded, 16)
            act.dma_start(wout[:, 0:2, :], w_out[0:2 * P, :].rearrange("(m p) c -> p m c", p=P)).then_inc(weights_loaded, 16)
            act.dma_start(wout[0:CT[2][1], 2, :], w_out[2 * P:C, :]).then_inc(weights_loaded, 16)
            act.dma_start(mask_col[:, :], spatial_mask.rearrange("(s p) -> p s", p=P), allow_slow_non_contiguous=True).then_inc(late_loaded, 16)
            for b in range(B):
                act.dma_start(vw[HIP:HIP + 1, b, :], b_out.rearrange("(a c) -> a c", a=1)).then_inc(late_loaded, 16)
            act.wait_ge(ip_step, 1)
            nc.scalar.activation(ip_stat[:, 1:2], ip_stat[:, 0:1], ACT.Sqrt).then_inc(ip_root, 1)
            act.wait_ge(bank_filled[0], 1)
            nc.scalar.activation(ip_t, bank[0][:, 0:ET * ALLIP].rearrange("p (e i) -> p e i", e=ET), ACT.Copy)\
              .then_inc(bank_drained[0], 1)
            act.wait_ge(weights_loaded, 16 * 6)
            act.wait_ge(bank_filled[1], 1)
            nc.scalar.activation(wvx[:, :, C:C + ALLIP], bank[1][:, 0:ET * ALLIP].rearrange("p (e i) -> p e i", e=ET),
                                 ACT.Copy).then_inc(bank_drained[1], 1)

            for b in range(B):
                act.wait_ge(bank_filled[b], SETUP_USES[b])
                nc.scalar.activation(vw[0:HIP, b, :], bank[b][0:HIP, 0:C], ACT.Copy).then_inc(bank_drained[b], 1)

            with act.Fori(0, B) as b:
                for c, (c0, cn) in enumerate(CT):
                    j = XT_JOB[c]
                    act.wait_ge(bank_filled[j[0]], use(j, b))
                    nc.scalar.activation(x_t[0:cn, c, :], bank[j[0]][0:cn, 0:S], ACT.Copy).then_inc(bank_drained[j[0]], 1)
                for e in range(ET):
                    j = CT_JOB[e]
                    act.wait_ge(bank_filled[j[0]], use(j, b))
                    nc.scalar.activation(ctx_t[:, e, :], bank[j[0]][:, 0:T], ACT.Copy).then_inc(bank_drained[j[0]], 1)
                act.wait_ge(parts_saved, 1 + 16 * 2 * NC * b)
                for t in range(2 * NC):
                    j, c0, cn = (Q_JOB + K_JOB)[t], *CT[t % NC]
                    act.wait_ge(bank_filled[j[0]], use(j, b))
                    if t < NC:
                        nc.scalar.activation(q_full[0:cn, t, :], bank[j[0]][0:cn, 0:S], ACT.Copy).then_inc(q_full_ready, 1)
                        nc.scalar.activation(parts[0:cn, t, 0, 0:S], bank[j[0]][0:cn, 0:S], ACT.Copy).then_inc(hi_split, 1)
                    else:
                        nc.scalar.activation(parts[0:cn, t, 0, 0:T], bank[j[0]][0:cn, 0:T], ACT.Copy, scale=SCALE)\
                          .then_inc(hi_split, 1)
                act.wait_ge(v_saved, 1 + 16 * b)
                for k in range(TT):
                    j = V_JOB[k]
                    v_k = v_sb[:, :, k, :]
                    act.wait_ge(bank_filled[j[0]], use(j, b))
                    nc.scalar.activation(v_k[:, :, 0:D], bank[j[0]][0:TP, 0:C].rearrange("p (h d) -> p h d", d=D), ACT.Copy)
                    nc.scalar.activation(sem_raw[:, k, :], bank[j[0]][0:TP, bass.ds(b * N_IP + C, N_IP)], ACT.Copy)\
                      .then_inc(v_hi_split, 1)
                act.wait_ge(bank_filled[IPS_JOB[0]], use(IPS_JOB, b))
                apart(act)
                nc.scalar.activation(ip_scores[:, b].rearrange("p h s n -> p s h n"),
                                     bank[IPS_JOB[0]][:, 0:ST * HIP].rearrange("p (s h n) -> p s h n", s=ST, n=N_IP), ACT.Copy)\
                  .then_inc(bank_drained[IPS_JOB[0]], 1)
                act.wait_ge(bank_drained[SCALE_JOB[0]], use(SCALE_JOB, b))
                act.wait_ge(u_saved, 1 + 16 * b)
                for k in range(TT):
                    j, n = G_JOB[k], U_COLS[k]
                    act.wait_ge(bank_filled[j[0]], use(j, b))
                    apart(act)
                    nc.scalar.activation(u_sb[:, 1, GH[k] + k * TP:GH[k] + T], bank[j[0]][0:TP, 0:n], ACT.Identity,
                                         scale=scale[0:TP, b, 0:1]).then_inc(gram_hi_split, 1)
                    if n > TP:
                        if k >= 2:
                            act.wait_ge(bank_drained[G_JOB[k - 2][0]], use(G_JOB[k - 2], b))
                            apart(act)
                        nc.scalar.activation(gram_hi2[:, k % 2, 0:n - TP], bank[j[0]][0:TP, TP:n], ACT.Identity,
                                             scale=scale[0:TP, b, 1:2]).then_inc(gram_hi2_split, 1)
                act.wait_ge(bank_filled[GT_JOB[0]], use(GT_JOB, b))
                for k in range(1, TT):
                    src = bank16(GT_JOB[0])[0:TP, GT_COL[k]:GT_COL[k] + k * P].rearrange("p (i t) -> p i t", t=P)[:, :, 0:TP]
                    last = nc.scalar.activation(u_sb[:, 1, GH[k]:GH[k] + k * TP].rearrange("p (i t) -> p i t", t=TP), src, ACT.Copy)
                last.then_inc(bank_drained[GT_JOB[0]], 1)

            def exp(v, st, free):
                act.wait_ge(row_max_found, v + 1)
                if free:
                    act.wait_ge(norms_done, v - 1)
                nc.scalar.activation(probs[:, st, :], bank[S_BANK + st % 2][:, 0:T], ACT.Exp, bias=neg_max[:, st:st + 1])\
                  .then_inc(probs_ready, 1)

            def halve(v, st):
                act.wait_ge(probs_ready, v + 1)
                act.wait_ge(weight_ready, v + 1)
                nc.scalar.activation(half_hi[:, st % 2, :], probs[:, st, :], ACT.Copy, scale=0.5).then_inc(half_ready, 1)

            def hi(v, par):
                act.wait_ge(probs_t_filled, v + 1)
                nc.scalar.activation(probs_hi[:, par, :], bank[PT_BANK + par][0:TP, 0:S], ACT.Copy, scale=PROB_SCALE)\
                  .then_inc(hi_ready, 1)

            def drain_out(g, pair, slot):
                act.wait_ge(out_filled, 2 * g + pair + 1)
                act.wait_ge(head_reduced, g + 1)
                nc.scalar.activation(out_raw[:, 2 * slot + pair].rearrange("p u c -> p (u c)"),
                                     bank[O_BANK + pair][:, 0:2 * VCOLS], ACT.Copy).then_inc(out_drained, 1)

            def head_steps(g, slot, first):
                for j in range(ST):
                    if not (first and j < 2):
                        hi(ST * g + j - 1, (j - 1) % 2)
                    exp(ST * g + j, j, not first)
                    if first and j == 1:
                        hi(0, 0)
                    halve(ST * g + j, j)
                    if j % 2 == 0 and not first:
                        drain_out(g - 1, j // 2, (slot - 1) % 2)

            head_steps(0, 0, True)
            head_steps(1, 1, False)
            with act.Fori(1, HEADS // 2) as g2:
                for slot in range(2):
                    head_steps(2 * g2 + slot, slot, False)
            hi(UNITS - 1, (ST - 1) % 2)
            for pair in range(2):
                drain_out(HEADS - 1, pair, 1)

            act.wait_ge(square_ready, 1)
            nc.scalar.activation(root, square, ACT.Sqrt).then_inc(root_ready, 1)

            def step(b, par):
                act.wait_ge(ip_fused, b + 1)
                nc.scalar.activation(ip_exp, fused, ACT.Exp, scale=SEM_SCALE).then_inc(ip_exp_ready, 1)
                for c, (c0, cn) in enumerate(CT):
                    act.wait_ge(text_t_filled, (NC + 1) * b + c + 1)
                    nc.scalar.activation(text_t[0:cn, par, c, :], bank[c][0:cn, 0:S], ACT.Copy).then_inc(text_t_ready, 1)
                act.wait_ge(text_t_filled, (NC + 1) * b + NC + 1)
                nc.scalar.activation(ip_probs_t[0:HIP, par, :], bank[NC][0:HIP, 0:S], ACT.Copy).then_inc(text_t_ready, 1)

            with act.Fori(0, B // 2) as pair:
                for par in range(2):
                    step(2 * pair + par, par)

        @block.vector
        def _(dve):
            dve.sem_inc(norms_done, 2)
            dve.sem_inc(out_drained, 2)
            dve.wait_ge(ip_loaded, 16 * B)
            nc.vector.scalar_tensor_tensor(discard[0:ALLIP, 0, :], ip_rows[:, 0, :], 1.0, ip_rows[:, 0, :], ALU.mult, ALU.mult,
                                           accum_out=ip_stat[:, 0:1]).then_inc(ip_step, 1)
            dve.wait_ge(ip_root, 1)
            nc.vector.tensor_scalar(ip_stat[:, 2:3], ip_stat[:, 1:2], 1e-18, None, ALU.max).then_inc(ip_step, 1)
            dve.wait_ge(ip_step, 2)
            nc.vector.reciprocal(ip_stat[:, 3:4], ip_stat[:, 2:3]).then_inc(ip_step, 1)
            dve.wait_ge(ip_step, 3)
            nc.vector.scalar_tensor_tensor(ip_stat[:, 4:5], ip_stat[:, 0:1], ip_stat[:, 3:4], ip_stat[:, 2:3], ALU.mult,
                                           ALU.add).then_inc(ip_step, 1)
            dve.wait_ge(ip_step, 4)
            nc.vector.tensor_scalar(ip_stat[:, 5:6], ip_stat[:, 4:5], 0.5, EPS, ALU.mult, ALU.max).then_inc(ip_step, 1)
            dve.wait_ge(ip_step, 5)
            nc.vector.reciprocal(ip_stat[:, 6:7], ip_stat[:, 5:6]).then_inc(ip_step, 1)
            dve.wait_ge(ip_step, 6)
            nc.vector.tensor_scalar(ip_rows[:, 1, :], ip_rows[:, 0, :], ip_stat[:, 6:7], None, ALU.mult).then_inc(ip_step, 1)
            dve.wait_ge(consts_made, CONSTS)
            for j, bd, n_last in ((2, kip_bd, 0), (3, vip_bd, 1)):
                dve.wait_ge(bank_filled[j], 1)
                for m, (c0, cn) in enumerate(CT):
                    src = bank[j][0:cn, m * ALLIP:(m + 1) * ALLIP].rearrange("p (b n) -> p b n", b=B)
                    last = nc.vector.tensor_tensor(
                        bd[0:cn, m].rearrange("p b (h n) -> p b h n", n=N_IP),
                        src.unsqueeze(2).broadcast_to([cn, B, H, N_IP]),
                        headmask[0:cn, m, :].unsqueeze(1).unsqueeze(3).broadcast_to([cn, B, H, N_IP]), ALU.mult)
                last.then_inc(bank_drained[j], 1)

            with dve.Fori(0, B) as b:
                dve.wait_ge(ctx_loaded, 16 * (b + 1))
                for k in range(TT):
                    if k >= 2:
                        dve.wait_ge(sumsq_ready, TT * b + k - 1)
                    nc.vector.scalar_tensor_tensor(discard[0:TP, k % 2, :], ctx_sb[:, k, :], 1.0, ctx_sb[:, k, :], ALU.mult, ALU.mult,
                                                   accum_out=sumsq[:, k:k + 1]).then_inc(sumsq_ready, 1)
                dve.wait_ge(sumsq_ready, TT * (b + 1))
                nc.vector.tensor_reduce(row_max[:, :], sumsq[:, :], AX.X, ALU.max).then_inc(row_max_ready, 1)
                dve.wait_ge(bank_filled[TOP_JOB[0]], use(TOP_JOB, b))
                nc.vector.tensor_reduce(top[:, 0:1], bank[TOP_JOB[0]][0:1, 0:TP], AX.X, ALU.max)\
                  .then_inc(bank_drained[TOP_JOB[0]], 1)
                dve.wait_ge(bank_drained[TOP_JOB[0]], use(TOP_JOB, b))
                nc.vector.tensor_scalar(scale_row[:, 2:3], top[:, 0:1], TINY, 2.0, ALU.max, ALU.mult).then_inc(scale_step, 1)
                dve.wait_ge(scale_step, 2 * b + 1)
                nc.vector.reciprocal(top[:, 1:2], scale_row[:, 2:3]).then_inc(scale_step, 1)
                dve.wait_ge(scale_step, 2 * b + 2)
                nc.vector.tensor_scalar(scale_row[:, 0:1], top[:, 1:2], 2.0 * GRAM_TOP, None, ALU.mult).then_inc(scale_row_ready, 1)
                nc.vector.tensor_scalar(scale_row[:, 1:2], top[:, 1:2], 4.0 * GRAM_TOP, None, ALU.mult).then_inc(scale_row_ready, 1)

                def residual(t):
                    j, c0, cn = (Q_JOB + K_JOB)[t], *CT[t % NC]
                    n = S if t < NC else T
                    dve.wait_ge(hi_split, 2 * NC * b + t + 1)
                    dve.wait_ge(parts_split, 2 * NC * b + t + 1)
                    nc.vector.scalar_tensor_tensor(resid[0:cn, t % R1, 0:n], bank[j[0]][0:cn, 0:n], 1.0 if t < NC else SCALE,
                                                   parts[0:cn, t, 0, 0:n], ALU.mult, ALU.subtract)\
                      .then_inc(bank_drained[j[0]], 1)

                for t in range(NC):
                    residual(t)
                dve.wait_ge(bank_filled[SCALE_JOB[0]], use(SCALE_JOB, b))
                nc.vector.tensor_copy(scale[:, b, :], bank[SCALE_JOB[0]][:, 0:3]).then_inc(bank_drained[SCALE_JOB[0]], 1)
                for t in range(NC, 2 * NC):
                    residual(t)
                for k in range(TT):
                    j = V_JOB[k]
                    v_k = v_sb[:, :, k, :]
                    dve.wait_ge(v_hi_split, TT * b + k + 1)
                    dve.wait_ge(v_split, TT * b + k + 1)
                    nc.vector.tensor_tensor(resid_v[:, k % RV, :].rearrange("p (h d) -> p h d", d=D),
                                            bank[j[0]][0:TP, 0:C].rearrange("p (h d) -> p h d", d=D), v_k[:, :, 0:D],
                                            ALU.subtract).then_inc(bank_drained[j[0]], 1)
                dve.wait_ge(bank_drained[SCALE_JOB[0]], use(SCALE_JOB, b))
                for k in range(TT):
                    j, n = G_JOB[k], U_COLS[k]
                    gram = bank[j[0]]
                    dve.wait_ge(gram_hi_split, TT * b + k + 1)
                    if n > TP:
                        dve.wait_ge(gram_hi2_split, (TT - 1) * b + k + 1)
                        nc.vector.scalar_tensor_tensor(u_sb[:, 1, UL[k] + TP:UL[k] + n], gram[0:TP, TP:n],
                                                       scale[0:TP, b, 1:2], gram_hi2[:, k % 2, 0:n - TP],
                                                       ALU.mult, ALU.subtract)
                    nc.vector.scalar_tensor_tensor(u_sb[:, 1, UL[k]:UL[k] + TP], gram[0:TP, 0:TP],
                                                   scale[0:TP, b, 0:1], u_sb[:, 1, GH[k] + k * TP:GH[k] + (k + 1) * TP],
                                                   ALU.mult, ALU.subtract).then_inc(bank_drained[j[0]], 1)

            def row_maximum(v, st):
                dve.wait_ge(scores_filled, v + 1)
                nc.vector.tensor_reduce(neg_max[:, st:st + 1], bank[S_BANK + st % 2][:, 0:T], AX.X, ALU.max, negate=True)\
                  .then_inc(row_max_found, 1)

            def norm(v, st):
                dve.wait_ge(quad_filled, v + 1)
                dve.wait_ge(weight_ready, 2 + v + 1)
                nc.vector.scalar_tensor_tensor(discard[:, st % 2, 0:T], bank[Y_BANK + st % 2][:, 0:T], 1.0, weight[:, st % 2, :], ALU.mult,
                                               ALU.mult, accum_out=norms[:, bass.ds(v, 1)]).then_inc(norms_done, 1)

            def lo(v, par):
                dve.wait_ge(hi_ready, v + 1)
                nc.vector.scalar_tensor_tensor(probs_lo[:, par, :], bank[PT_BANK + par][0:TP, 0:S], PROB_SCALE,
                                               probs_hi[:, par, :], ALU.mult, ALU.subtract).then_inc(lo_ready, 1)

            def head_steps(g, first):
                for j in range(ST):
                    row_maximum(ST * g + j, j)
                    if not (first and j < 3):
                        norm(ST * g + j - 3, (j - 3) % ST)
                    if not (first and j == 0):
                        lo(ST * g + j - 1, (j - 1) % 2)

            head_steps(0, True)
            with dve.Fori(1, HEADS) as g:
                head_steps(g, False)
            norm(UNITS - 3, (UNITS - 3) % ST)
            lo(UNITS - 1, (UNITS - 1) % 2)
            norm(UNITS - 2, (UNITS - 2) % ST)
            norm(UNITS - 1, (UNITS - 1) % ST)

            dve.wait_ge(head_reduced, 2 + HEADS)
            dve.wait_ge(norms_done, 2 + UNITS)
            nc.vector.scalar_tensor_tensor(square.rearrange("p (b u) -> p b u", b=B),
                                           norms[:, :].rearrange("p (b u) -> p b u", b=B), 0.0,
                                           scale[:, :, 2].unsqueeze(2).broadcast_to([P, B, U]),
                                           ALU.max, ALU.mult).then_inc(square_ready, 1)
            dve.wait_ge(late_loaded, 16 * (1 + B))
            dve.wait_ge(root_ready, 1)

            fused3 = fused.rearrange("p (u n) -> p u n", n=N_IP)
            exp3 = ip_exp.rearrange("p (u n) -> p u n", n=N_IP)
            stat, stat2 = ip_stat3[:, 0:U], ip_stat3[:, U:2 * U]

            def over_tokens(a):
                return a.unsqueeze(2).broadcast_to([P, U, N_IP])

            ELEM = 13

            def elem(b, par, free):
                step = ELEM * b
                done = [0]

                def then(ins):
                    ins.then_inc(elem_step, 1)
                    done[0] += 1
                    dve.wait_ge(elem_step, step + done[0])

                sums = reduced[:, bass.ds(b * H, H), :, RCOLS - 1].rearrange("p h s -> p (h s)")
                if free:
                    dve.wait_ge(text_ready, b - 1)
                    apart(dve)
                nc.vector.reciprocal(inv_sum[:, par, :], sums).then_inc(inv_sum_ready, 1)
                guard, inv_guard, ratio, twice, least, norm_b, inv_norm = norm_tmp
                root_b, square_b = root[:, bass.ds(b * U, U)], square[:, bass.ds(b * U, U)]
                then(nc.vector.tensor_scalar(guard, root_b, 1e-18, None, ALU.max))
                then(nc.vector.reciprocal(inv_guard, guard))
                then(nc.vector.tensor_tensor(ratio, square_b, inv_guard, ALU.mult))
                then(nc.vector.tensor_tensor(twice, ratio, guard, ALU.add))
                then(nc.vector.tensor_scalar(least, sums, EPS, None, ALU.mult))
                then(nc.vector.scalar_tensor_tensor(norm_b, twice, 0.5, least, ALU.mult, ALU.max))
                then(nc.vector.reciprocal(inv_norm, norm_b))
                red_b = reduced[:, bass.ds(b * H, H), :, D:D + N_IP].rearrange("p h s n -> p (h s) n")
                then(nc.vector.tensor_tensor(fused3, red_b, over_tokens(inv_norm), ALU.mult))
                then(nc.vector.scalar_tensor_tensor(fused, ip_scores[:, b].rearrange("p h s n -> p (h s n)"), SCALE / SEM_SCALE,
                                                    fused, ALU.mult, ALU.add))
                then(nc.vector.tensor_reduce(stat, fused3, AX.X, ALU.max))
                nc.vector.tensor_tensor(fused3, fused3, over_tokens(stat), ALU.subtract).then_inc(ip_fused, 1)
                dve.wait_ge(ip_exp_ready, b + 1)
                then(nc.vector.tensor_reduce(stat, exp3, AX.X, ALU.add))
                then(nc.vector.reciprocal(stat2, stat))
                then(nc.vector.tensor_tensor(stat.rearrange("p (h s) -> p h s", s=ST), stat2.rearrange("p (h s) -> p h s", s=ST),
                                             mask_col[:, :].unsqueeze(1).broadcast_to([P, H, ST]), ALU.mult))
                assert done[0] == ELEM
                if free:
                    dve.wait_ge(text_t_filled, (NC + 1) * (b - 1))
                nc.vector.tensor_tensor(ip_probs[:, par].rearrange("p s (h n) -> p h s n", n=N_IP),
                                        exp3.rearrange("p (h s) n -> p h s n", s=ST),
                                        stat.rearrange("p (h s) -> p h s", s=ST).unsqueeze(3).broadcast_to([P, H, ST, N_IP]),
                                        ALU.mult).then_inc(ip_probs_ready, 1)

            def residual_add(b, half, par, free=True):
                dve.wait_ge(x_reloaded[par], 16 * (half + 1))
                for s in range(ST):
                    dve.wait_ge(y_filled, ST * b + s + 1)
                    if free:
                        dve.wait_ge(y_stored, 16 * ST * b)
                    nc.vector.tensor_tensor(y_sb[:, s, :], bank[4 + s][:, 0:C], x_sb[:, par, s, :], ALU.add)\
                      .then_inc(y_ready, 1)

            elem(0, 0, False)
            elem(1, 1, False)
            elem(2, 0, True)
            residual_add(0, 0, 0, False)
            elem(3, 1, True)
            residual_add(1, 0, 1)
            with dve.Fori(2, B // 2) as pair:
                elem(2 * pair, 0, True)
                residual_add(2 * pair - 2, pair - 1, 0)
                elem(2 * pair + 1, 1, True)
                residual_add(2 * pair - 1, pair - 1, 1)
            residual_add(B - 2, B // 2 - 1, 0)
            residual_add(B - 1, B // 2 - 1, 1)

        @block.tensor
        def _(pe):
            pe.wait_ge(consts_made, CONSTS)
            pe.wait_ge(ip_loaded, 16 * B)
            for e in range(ET):
                last = nc.tensor.transpose(bank[0][:, e * ALLIP:(e + 1) * ALLIP], ip_rows[:, 0, e * P:(e + 1) * P],
                                           ident[0:ALLIP, 0:ALLIP])
            last.then_inc(bank_filled[0], 1)
            pe.wait_ge(ip_weights_loaded, 32)
            pe.wait_ge(bank_drained[0], 1)
            for j, w in ((2, wk_ip), (3, wv_ip)):
                for m, (c0, cn) in enumerate(CT):
                    for e in range(ET):
                        last = nc.tensor.matmul(bank[j][0:cn, m * ALLIP:(m + 1) * ALLIP], w[:, e, c0:c0 + cn], ip_t[:, e, :],
                                                start=(e == 0), stop=(e == ET - 1))
                last.then_inc(bank_filled[j], 1)
            pe.wait_ge(ip_step, 7)
            for e in range(ET):
                last = nc.tensor.transpose(bank[1][:, e * ALLIP:(e + 1) * ALLIP], ip_rows[:, 1, e * P:(e + 1) * P],
                                           ident[0:ALLIP, 0:ALLIP])
            last.then_inc(bank_filled[1], 1)
            pe.wait_ge(weights_loaded, 16 * 6)
            pe.wait_ge(bank_drained[3], 1)
            for b in range(B):
                pe.wait_ge(bank_drained[b], SETUP_USES[b] - 1)
                for c, (r0, rn) in enumerate(CT):
                    last = nc.tensor.matmul(bank[b][0:HIP, 0:C], vip_bd[0:rn, c, b, :], wout[0:rn, c, :],
                                            start=(c == 0), stop=(c == NC - 1))
                last.then_inc(bank_filled[b], 1)

            with pe.Fori(0, B) as b:
                def free(job):
                    pe.wait_ge(bank_drained[job[0]], use(job, b) - 1)

                pe.wait_ge(x_loaded, 16 * (b + 1))
                for j in XT_JOB:
                    free(j)
                for c, (c0, cn) in enumerate(CT):
                    j = XT_JOB[c]
                    for s in range(ST):
                        last = nc.tensor.transpose(bank[j[0]][0:cn, s * P:(s + 1) * P], x_sb[:, 0, s, c0:c0 + cn], ident[:, :])
                    last.then_inc(bank_filled[j[0]], 1)
                pe.wait_ge(ctx_loaded, 16 * (b + 1))
                for e in range(ET):
                    j = CT_JOB[e]
                    free(j)
                    for k in range(TT):
                        last = nc.tensor.transpose(bank[j[0]][:, k * TP:(k + 1) * TP], ctx_sb[:, k, e * P:(e + 1) * P],
                                                   ident[0:TP, 0:TP])
                    last.then_inc(bank_filled[j[0]], 1)
                free(TOP_JOB)
                pe.wait_ge(row_max_ready, b + 1)
                nc.tensor.transpose(bank[TOP_JOB[0]][0:1, 0:TP], row_max[:, :], ident[0:TP, 0:TP])\
                  .then_inc(bank_filled[TOP_JOB[0]], 1)
                for m, (c0, cn) in enumerate(CT):
                    j = Q_JOB[m]
                    pe.wait_ge(bank_drained[XT_JOB[-1][0]], use(XT_JOB[-1], b))
                    free(j)
                    for c, (r0, rn) in enumerate(CT):
                        last = nc.tensor.matmul(bank[j[0]][0:cn, 0:S], wq[0:rn, c, c0:c0 + cn], x_t[0:rn, c, :],
                                                start=(c == 0), stop=(c == NC - 1))
                    last.then_inc(bank_filled[j[0]], 1)
                free(SCALE_JOB)
                pe.wait_ge(scale_row_ready, 2 * (b + 1))
                nc.tensor.matmul(bank[SCALE_JOB[0]][:, 0:3], ones_row[:, :], scale_row[:, :], start=True, stop=True)\
                  .then_inc(bank_filled[SCALE_JOB[0]], 1)
                pe.wait_ge(bank_drained[CT_JOB[-1][0]], use(CT_JOB[-1], b))
                for m, (c0, cn) in enumerate(CT):
                    j = K_JOB[m]
                    free(j)
                    for e in range(ET):
                        last = nc.tensor.matmul(bank[j[0]][0:cn, 0:T], wk[:, e, c0:c0 + cn], ctx_t[:, e, :],
                                                start=(e == 0), stop=(e == ET - 1))
                    last.then_inc(bank_filled[j[0]], 1)
                pe.wait_ge(bank_drained[1], 1)
                for k in range(TT):
                    j = V_JOB[k]
                    free(j)
                    for e in range(ET):
                        last = nc.tensor.matmul(bank[j[0]][0:TP, 0:C + ALLIP], ctx_t[:, e, k * TP:(k + 1) * TP], wvx[:, e, :],
                                                start=(e == 0), stop=(e == ET - 1))
                    last.then_inc(bank_filled[j[0]], 1)
                free(IPS_JOB)
                pe.wait_ge(q_full_ready, NC * (b + 1))
                pe.wait_ge(bank_drained[2], 1)
                for s in range(ST):
                    for c, (r0, rn) in enumerate(CT):
                        last = nc.tensor.matmul(bank[IPS_JOB[0]][:, s * HIP:(s + 1) * HIP], q_full[0:rn, c, s * P:(s + 1) * P],
                                                kip_bd[0:rn, c, b, :], start=(c == 0), stop=(c == NC - 1))
                last.then_inc(bank_filled[IPS_JOB[0]], 1)
                for k in range(TT):
                    j = G_JOB[k]
                    free(j)
                    for e in range(ET):
                        last = nc.tensor.matmul(bank[j[0]][0:TP, 0:U_COLS[k]], ctx_t[:, e, k * TP:(k + 1) * TP],
                                                ctx_t[:, e, k * TP:T], start=(e == 0), stop=(e == ET - 1))
                    last.then_inc(bank_filled[j[0]], 1)
                free(GT_JOB)
                pe.wait_ge(gram_hi_split, TT * b + TT - 1)
                for k in range(1, TT):
                    for i in range(k):
                        last = nc.tensor.transpose(bank16(GT_JOB[0])[0:TP, GT_COL[k] + i * P:GT_COL[k] + i * P + TP],
                                                   u_sb[:, 1, GH[i] + k * TP:GH[i] + (k + 1) * TP], ident16[0:TP, 0:TP])
                last.then_inc(bank_filled[GT_JOB[0]], 1)

            for j in range(8):
                pe.wait_ge(bank_drained[j], end_of_phase1(j))

            def scores(r, st, blk, u, free):
                if st == 0:
                    pe.wait_ge(head_loaded[r], 16 * 10 * (blk + 1))
                if free:
                    pe.wait_ge(probs_ready, u - 1)
                nc.tensor.matmul(bank[S_BANK + st % 2][:, 0:T], q_ring[:, r, st * P:(st + 1) * P], k_ring[:, r, :],
                                 start=True, stop=True).then_inc(scores_filled, 1)

            def transposes(st, u):
                pe.wait_ge(probs_ready, u + 1)
                for k in range(TT):
                    last = nc.tensor.transpose(bank[PT_BANK + st % 2][0:TP, k * P:(k + 1) * P],
                                               probs[:, st, k * TP:(k + 1) * TP], ident[:, :])
                last.then_inc(probs_t_filled, 1)

            def unit(j, u, blk, par, ahead):
                r, st = j // ST, j % ST
                y, o = bank[Y_BANK + st % 2][:, 0:T], bank[O_BANK + st // 2][:, (st % 2) * VCOLS:(st % 2 + 1) * VCOLS]

                if ahead > 1:
                    scores((j + 2) // ST % RING, (st + 2) % ST, blk + (j + 2) // BLK, u + 2, True)
                if ahead > 0:
                    transposes((st + 1) % ST, u + 1)
                pe.wait_ge(hi_ready, u + 1)
                pe.wait_ge(norms_done, u + 1)
                if st % 2 == 0:
                    pe.wait_ge(out_drained, BLK // 2 * blk + j // 2 + 1)
                for k in range(TT):
                    hi_k = probs_hi[:, st % 2, k * P:(k + 1) * P]
                    nc.tensor.matmul(o, hi_k, v_ring[:, r, k, :], start=(k == 0), stop=False)
                    nc.tensor.matmul(y, hi_k, u_sb[:, par, GH[k]:GH[k] + T], start=(k == 0), stop=False)
                    last = nc.tensor.matmul(y[:, k * TP:T], hi_k, u_sb[:, par, UL[k]:UL[k] + U_COLS[k]], start=False,
                                            stop=(k == TT - 1))
                last.then_inc(quad_filled, 1)
                pe.wait_ge(lo_ready, u + 1)
                for k in range(TT):
                    last = nc.tensor.matmul(o, probs_lo[:, st % 2, k * P:(k + 1) * P], v_ring[:, r, k, :], start=False,
                                            stop=(k == TT - 1))
                if st % 2 == 1:
                    last.then_inc(out_filled, 1)

            def heads(blk, par, last):
                for j in range(BLK):
                    unit(j, BLK * blk + j, blk, par, BLK - 1 - j if last else 2)

            scores(0, 0, 0, 0, False)
            scores(0, 1, 0, 1, False)
            transposes(0, 0)
            with pe.Fori(0, B // 2 - 1) as pair:
                for par in range(2):
                    pe.wait_ge(u_loaded, 16 * (2 * pair + par + 1))
                    apart(pe)
                    with pe.Fori(0, BLOCKS) as i:
                        heads(BLOCKS * (2 * pair + par) + i, par, False)
            pe.wait_ge(u_loaded, 16 * (B - 1))
            with pe.Fori(0, BLOCKS) as i:
                heads(BLOCKS * (B - 2) + i, 0, False)
            pe.wait_ge(u_loaded, 16 * B)
            with pe.Fori(0, BLOCKS - 1) as i:
                heads(BLOCKS * (B - 1) + i, 1, False)
            heads(BLOCKS * B - 1, 1, True)

            pe.wait_ge(norms_done, 2 + UNITS)
            pe.wait_ge(out_drained, 2 + 2 * HEADS)

            def text_transposes(b, par, free):
                pe.wait_ge(text_ready, b + 1)
                if free:
                    pe.wait_ge(text_t_ready, (NC + 1) * b)
                for c, (c0, cn) in enumerate(CT):
                    for s in range(ST):
                        last = nc.tensor.transpose(bank[c][0:cn, s * P:(s + 1) * P], text[:, par, s, c0:c0 + cn], ident[:, :])
                    last.then_inc(text_t_filled, 1)
                pe.wait_ge(ip_probs_ready, b + 1)
                for s in range(ST):
                    last = nc.tensor.transpose(bank[NC][0:HIP, s * P:(s + 1) * P], ip_probs[:, par, s, :], ident[:, :])
                last.then_inc(text_t_filled, 1)

            def project(b, par, free):
                pe.wait_ge(text_t_ready, (NC + 1) * (b + 1))
                for s in range(ST):
                    if free:
                        pe.wait_ge(y_ready, ST * (b - 1) + s + 1)
                    y = bank[4 + s][:, 0:C]
                    for c, (c0, cn) in enumerate(CT):
                        nc.tensor.matmul(y, text_t[0:cn, par, c, s * P:(s + 1) * P], wout[0:cn, c, :], start=(c == 0), stop=False)
                    nc.tensor.matmul(y, ip_probs_t[0:HIP + 1, par, s * P:(s + 1) * P], vw[0:HIP + 1, b, :], start=False,
                                     stop=True).then_inc(y_filled, 1)

            pe.wait_ge(late_loaded, 16 * (1 + B))
            text_transposes(0, 0, False)
            text_transposes(1, 1, True)
            project(0, 0, False)
            with pe.Fori(1, B // 2) as pair:
                text_transposes(2 * pair, 0, True)
                project(2 * pair - 1, 1, True)
                text_transposes(2 * pair + 1, 1, True)
                project(2 * pair, 0, True)
            project(B - 1, 1, True)


INPUTS = ["x", "ctx_2048", "fside_S_0", "L0_xattn_W_q", "L0_xattn_W_k", "L0_xattn_W_v", "L0_xattn_W_k_ip",
          "L0_xattn_W_v_ip", "L0_xattn_W_out", "L0_xattn_b_out"]


def kernel(**inputs):
    import numpy as np
    import concourse.bacc as bacc
    from concourse import mybir
    from concourse.bass_utils import run_bass_kernel_spmd

    nc = bacc.Bacc("TRN2", target_bir_lowering=False, num_devices=1)
    arrays, args = {}, []
    for name in INPUTS:
        a = np.ascontiguousarray(inputs[name])
        arrays[f"in_{name}"] = a
        args.append(nc.dram_tensor(f"in_{name}", a.shape, mybir.dt.from_np(a.dtype), kind="ExternalInput").ap())
    args.append(nc.dram_tensor("result", inputs["x"].shape, mybir.dt.float32, kind="ExternalOutput").ap())
    xattn_kernel(nc, *args)
    r = run_bass_kernel_spmd(nc, [arrays], core_ids=[0])
    return r.results[0]["result"]
```

```python
import concourse.bass as bass
from concourse import mybir
from contextlib import ExitStack


def xattn_kernel(
    nc: bass.Bass,
    x: bass.AP,
    ctx: bass.AP,
    spatial_mask: bass.AP,
    w_q: bass.AP,
    w_k: bass.AP,
    w_v: bass.AP,
    w_k_ip: bass.AP,
    w_v_ip: bass.AP,
    w_out: bass.AP,
    b_out: bass.AP,
    out: bass.AP,
):
    fp32 = mybir.dt.float32
    fp16 = mybir.dt.float16
    bf16 = mybir.dt.bfloat16
    ALU = mybir.AluOpType
    ACT = mybir.ActivationFunctionType
    AX = mybir.AxisListType

    B, S, C = x.shape
    E = ctx.shape[2]
    N_IP = 4
    T = ctx.shape[1] - N_IP
    H = 20
    D = C // H
    SCALE = float(D) ** -0.5
    SEM_SCALE = 0.5
    EPS = 1e-12
    TINY = 1e-30
    P = 128
    ST = S // P
    TT = 4
    TP = T // TT
    ET = E // P
    CT = [(c, min(P, C - c)) for c in range(0, C, P)]
    NC = len(CT)
    HIP = H * N_IP
    ALLIP = B * N_IP
    PROB_SCALE = 2.0 ** 14
    GRAM_TOP = 2.0 ** 14
    VW_PART = D + N_IP
    VCOLS = 2 * VW_PART + 1
    RCOLS = VW_PART + 1
    U_COLS = [T - TP * k for k in range(TT)]
    GH = [T * k for k in range(TT)]
    UL = [T * TT + sum(U_COLS[:k]) for k in range(TT)]
    U_ALL = T * TT + sum(U_COLS)
    PAIRS = [(0, 0), (1, 0), (2, 0), (0, 1), (1, 1), (0, 2)]
    KS = len(PAIRS) * D
    HEADS = B * H
    UNITS = HEADS * ST
    RING = 4
    BLK = RING * ST
    BLOCKS = H // RING

    q_parts = nc.dram_tensor("q_parts", [B, 3, C, S], bf16).ap()
    k_parts = nc.dram_tensor("k_parts", [B, 3, C, T], bf16).ap()
    v_parts = nc.dram_tensor("v_parts", [B, H, TP, TT * VCOLS], fp16).ap()
    u_parts = nc.dram_tensor("u_parts", [B, TP, U_ALL], fp16).ap()

    stack = ExitStack()
    with stack:
        def sb(name, shape, dt):
            return stack.enter_context(nc.sbuf_tensor(name, shape, dt))

        def sem(name):
            return stack.enter_context(nc.semaphore(name))

        ident = sb("ident", [P, P], fp32)
        ident16 = sb("ident16", [P, P], fp16)
        ones_row = sb("ones_row", [1, P], fp32)
        headmask = sb("headmask", [P, NC, H], fp32)
        mask_col = sb("mask_col", [P, ST], fp32)
        wq = sb("wq", [P, 2, NC, C], fp16)
        wk = sb("wk", [P, 2, ET, C], fp16)
        wvx = sb("wvx", [P, 2, ET, C + N_IP], fp16)
        wout = sb("wout", [P, NC, C], fp32)
        kip_bd = sb("kip_bd", [P, NC, B, HIP], fp32)
        ip_scores = sb("ip_scores", [P, B, H, ST, N_IP], fp32)
        vip = sb("vip", [P, NC, ALLIP], fp32)
        vw = sb("vw", [96, B, C], fp32)
        scale = sb("scale", [P, 4], fp32)
        kept_scale = sb("kept_scale", [P, B, 2], fp32)
        reduced = sb("reduced", [P, HEADS, ST, RCOLS], fp32)
        norms = sb("norms", [P, UNITS], fp32)
        x_sb = sb("x_sb", [P, 2, ST, C], fp32)
        u_sb = sb("u_sb", [TP, 2, U_ALL], fp16)
        v_ring = sb("v_ring", [TP, RING, TT, VCOLS], fp16)
        q_ring = sb("q_ring", [KS, RING, S], bf16)
        k_ring = sb("k_ring", [KS, RING, T], bf16)
        probs = sb("probs", [P, ST, T], fp32)
        half_hi = sb("half_hi", [P, 2, T], fp16)
        weight = sb("weight", [P, 2, T], fp32)
        neg_max = sb("neg_max", [P, ST], fp32)
        probs_hi = sb("probs_hi", [TP, 2, S], fp16)
        probs_lo = sb("probs_lo", [TP, 2, S], fp16)
        discard = sb("discard", [P, 2, E], fp32)
        out_raw = sb("out_raw", [P, 4, 2, VCOLS], fp32)
        v_sb = sb("v_sb", [TP, H, TT, VCOLS], fp16)
        work = sb("work", [P, 2 * NC * S], fp32)
        late = sb("late", [P, 2 * NC * 3 * S // 2], fp32)
        parts = late[:, :].bitcast(bf16).rearrange("p (t a s) -> p t a s", t=2 * NC, a=3)
        q_full = work[:, 0:NC * S].rearrange("p (c s) -> p c s", c=NC)
        resid = work[:, NC * S:2 * NC * S].rearrange("p (r s) -> p r s", r=3)
        sem_parts = sb("sem_parts", [TP, 2, TT, N_IP], fp16)
        gram_hi2 = sb("gram_hi2", [TP, 2, T - TP], fp16)
        sumsq = sb("sumsq", [P, TT + ST], fp32)
        row_max = sb("row_max", [P, 2], fp32)
        w_sums = sb("w_sums", [P, 3], fp32)
        w_scale = sb("w_scale", [P, 3], fp32)
        top = sb("top", [1, 2, 2], fp32)
        w_top = sb("w_top", [1, 3, 3], fp32)
        scale_row = sb("scale_row", [1, 5], fp32)
        w_row = sb("w_row", [1, 3], fp32)
        ip_stat = sb("ip_stat", [ALLIP, 8], fp32)
        spare = reduced[:, :, :, :].rearrange("p g s c -> p (g s c)")
        taken = [0]

        def carve(parts_n, n):
            a = spare[0:parts_n, taken[0]:taken[0] + n]
            taken[0] += n
            assert taken[0] <= HEADS * ST * RCOLS
            return a

        ctx_sb = carve(TP, TT * E).rearrange("p (k e) -> p k e", k=TT)
        ctx_t = carve(P, ET * T).bitcast(fp16).rearrange("p (a e t) -> p a e t", a=2, e=ET)
        x_t = carve(P, NC * S).bitcast(fp16).rearrange("p (a c s) -> p a c s", a=2, c=NC)
        wv_raw = carve(P, ET * C).rearrange("p (e c) -> p e c", e=ET)
        ipn_t = carve(P, ET * ALLIP).bitcast(fp16).rearrange("p (a e i) -> p a e i", a=2, e=ET)
        wk_ip = carve(P, ET * C).rearrange("p (e c) -> p e c", e=ET)
        wv_ip = carve(P, ET * C).rearrange("p (e c) -> p e c", e=ET)
        kip_batch = carve(P, NC * HIP).rearrange("p (m c) -> p m c", m=NC)
        ip_rows = carve(ALLIP, 2 * E).rearrange("p (a e) -> p a e", a=2)
        ip_t = carve(P, ET * ALLIP).rearrange("p (e i) -> p e i", e=ET)
        wk_raw = probs[:, :, :].rearrange("p s t -> p (s t)")[:, 0:ET * C].rearrange("p (e c) -> p e c", e=ET)
        wq_raw = weight[:, :, :].rearrange("p a t -> p (a t)")[:, 0:NC * C].rearrange("p (m c) -> p m c", m=NC)
        w_squares = [late[:, n * ET * C:(n + 1) * ET * C].rearrange("p (e c) -> p e c", c=C) for n in range(3)]
        ip_squares = late[0:ALLIP, 3 * ET * C:3 * ET * C + E]
        NS, U = 2 * ST * C, H * ST
        text = late[:, 0:NS].rearrange("p (a s c) -> p a s c", a=2, s=ST)
        square, root = (late[:, NS + n * UNITS:NS + (n + 1) * UNITS] for n in range(2))
        inv_sum = late[:, NS + 2 * UNITS:NS + 2 * UNITS + 2 * U].rearrange("p (a u) -> p a u", a=2)
        vip_bd = work[:, 0:NC * B * HIP].rearrange("p (m b c) -> p m b c", m=NC, b=B)
        text_t = work[:, :].rearrange("p (a c s) -> p a c s", a=2, c=NC)
        over_probs = probs[:, :, :].rearrange("p s t -> p (s t)")
        fused, ip_exp = (over_probs[:, n * ST * HIP:(n + 1) * ST * HIP] for n in range(2))
        norm_tmp = [over_probs[:, 2 * ST * HIP + n * U:2 * ST * HIP + (n + 1) * U] for n in range(7)]
        ip_stat3 = sb("ip_stat3", [P, 2 * ST * H], fp32)
        ip_probs_t = sb("ip_probs_t", [96, 2, S], fp32)
        over_kip = kip_bd[:, :, :, :].rearrange("p m b c -> p (m b c)")
        y_sb = over_kip[:, 0:ST * C].rearrange("p (s c) -> p s c", s=ST)
        ip_probs = over_kip[:, ST * C:ST * C + 2 * ST * HIP].rearrange("p (a s c) -> p a s c", a=2, s=ST)

        bank = [stack.enter_context(nc.psum_tensor(f"bank{j}", [P, 512], fp32)) for j in range(8)]
        def bank16(j):
            return bank[j][:, :].bitcast(fp16)

        GT_COL = [0, 0, P, 3 * P]
        S_BANK, PT_BANK, Y_BANK, O_BANK = 0, 2, 4, 6

        consts_made = sem("consts_made")
        unwatched = sem("unwatched")
        ip_loaded = sem("ip_loaded")
        ip_weights_loaded = sem("ip_weights_loaded")
        wq_loaded = sem("wq_loaded")
        wq_padded = sem("wq_padded")
        wk_loaded = sem("wk_loaded")
        wv_loaded = sem("wv_loaded")
        wout_loaded = sem("wout_loaded")
        w_sums_ready = sem("w_sums_ready")
        w_top_ready = sem("w_top_ready")
        w_root_ready = sem("w_root_ready")
        w_row_ready = sem("w_row_ready")
        w_hi_split = sem("w_hi_split")
        w_split = sem("w_split")
        top_ready = sem("top_ready")
        top_root_ready = sem("top_root_ready")
        in_hi_split = sem("in_hi_split")
        ipn_hi_split = sem("ipn_hi_split")
        ip_cols_ready = sem("ip_cols_ready")
        kip_ready = sem("kip_ready")
        vip_bd_ready = sem("vip_bd_ready")
        vw_filled = sem("vw_filled")
        vw_ready = sem("vw_ready")
        late_loaded = sem("late_loaded")
        ip_step = sem("ip_step")
        ip_root = sem("ip_root")
        bank_filled = [sem(f"bank_filled{j}") for j in range(8)]
        bank_drained = [sem(f"bank_drained{j}") for j in range(8)]
        x_loaded = sem("x_loaded")
        ctx_loaded = sem("ctx_loaded")
        x_reloaded = [sem(f"x_reloaded{par}") for par in range(2)]
        sumsq_ready = sem("sumsq_ready")
        row_max_ready = sem("row_max_ready")
        scale_row_ready = sem("scale_row_ready")
        q_full_ready = sem("q_full_ready")
        hi_split = sem("hi_split")
        mid_split = sem("mid_split")
        parts_split = sem("parts_split")
        parts_saved = sem("parts_saved")
        v_hi_split = sem("v_hi_split")
        sem_step = sem("sem_step")
        gram_hi_split = sem("gram_hi_split")
        gram_hi2_split = sem("gram_hi2_split")
        v_saved = sem("v_saved")
        u_saved = sem("u_saved")
        head_loaded = [sem(f"head_loaded{r}") for r in range(RING)]
        u_loaded = sem("u_loaded")
        scores_filled = sem("scores_filled")
        row_max_found = sem("row_max_found")
        probs_ready = sem("probs_ready")
        probs_t_filled = sem("probs_t_filled")
        hi_ready = sem("hi_ready")
        lo_ready = sem("lo_ready")
        quad_filled = sem("quad_filled")
        half_ready = sem("half_ready")
        weight_ready = sem("weight_ready")
        norms_done = sem("norms_done")
        out_filled = sem("out_filled")
        out_drained = sem("out_drained")
        head_reduced = sem("head_reduced")
        square_ready = sem("square_ready")
        root_ready = sem("root_ready")
        inv_sum_ready = sem("inv_sum_ready")
        elem_step = sem("elem_step")
        ip_fused = sem("ip_fused")
        ip_exp_ready = sem("ip_exp_ready")
        ip_probs_ready = sem("ip_probs_ready")
        text_ready = sem("text_ready")
        text_t_filled = sem("text_t_filled")
        text_t_ready = sem("text_t_ready")
        y_filled = sem("y_filled")
        y_ready = sem("y_ready")
        y_stored = sem("y_stored")

        FIRST_USES = [0, 0, 0, 0, 0, 0, 0, 4]
        IP_USES, IP_AFTER = [1, 1, 1, 1, 0, 0, 0, 0], 2
        USES = [3, 3, 3, 3, 3, 3, 3, 4]
        R1 = 3
        Q_JOB = [(0, 2), (1, 2), (2, 2)]
        XT_JOB = [(0, 1), (1, 1), (2, 1)]
        CT_JOB = [(3, 1), (4, 1), (5, 1), (6, 1)]
        TOP_JOB, SCALE_JOB = (7, 2), (7, 3)
        W_TOP, TOP_0, W_SCALE, SCALE_0 = (7, -3), (7, -2), (7, -1), (7, 0)
        K_JOB = [(3, 2), (4, 2), (5, 2)]
        V_JOB = [(6, 2), (2, 3), (0, 3), (1, 3)]
        IPS_JOB = (7, 1)
        G_JOB, GT_JOB = [(4, 3), (5, 3), (6, 3), (7, 4)], (3, 3)

        def use(job, b):
            j, n = job
            if isinstance(b, int) and b == 0:
                return FIRST_USES[j] + n + (IP_USES[j] if n > IP_AFTER else 0)
            return FIRST_USES[j] + IP_USES[j] + USES[j] * b + n

        def ip_use(j):
            return FIRST_USES[j] + IP_AFTER + 1

        def end_of_phase1(j):
            return FIRST_USES[j] + IP_USES[j] + USES[j] * B

        CTX_COL, X_COL, Q_COL, K_COL = range(4)
        V_DOWN, SEM_DOWN = 2.0 ** -16, 2.0 ** -13
        IN_TOP = 2.0 ** 14
        GRAM_SCALE = GRAM_TOP / IN_TOP ** 2
        SEM_SCALED = IN_TOP * SEM_DOWN
        SQUARE_SCALE = 2.0 * PROB_SCALE / GRAM_SCALE * SEM_SCALED ** 2
        SPLIT = [(0, 0), (0, 1), (1, 0)]
        IN_TILES = NC + ET

        CONSTS = 12

        def apart(eng):
            eng.sem_inc(unwatched, 1)

        block = stack.enter_context(nc.Block())

        @block.sync
        def _(sp):
            ctx_in = ctx[:, 0:T, :].rearrange("b (k p) e -> b p k e", p=TP)
            x_in = x.rearrange("b (s p) c -> b p s c", p=P)
            sp.dma_start(x_sb[:, 0], x_in[0]).then_inc(x_loaded, 16)
            sp.dma_start(ctx_sb, ctx_in[0]).then_inc(ctx_loaded, 16)
            for b in range(B):
                sp.dma_start(ip_rows[b * N_IP:(b + 1) * N_IP, 0, :], ctx[b, T:T + N_IP, :]).then_inc(ip_loaded, 16)
            sp.dma_start(wk_ip, w_k_ip.rearrange("(e p) c -> p e c", p=P)).then_inc(ip_weights_loaded, 16)
            sp.dma_start(wv_ip, w_v_ip.rearrange("(e p) c -> p e c", p=P)).then_inc(ip_weights_loaded, 16)

            def store_batch(b):
                for t in range(2 * NC):
                    c0, cn = CT[t % NC]
                    sp.wait_ge(parts_split, R1 + 2 * NC * b + t + 1)
                    dst = (q_parts if t < NC else k_parts)[b, :, c0:c0 + cn, :].rearrange("a c s -> c a s")
                    n = S if t < NC else T
                    sp.dma_start(dst, parts[0:cn, t, :, 0:n]).then_inc(parts_saved, 16)
                sp.wait_ge(sem_step, 2 * (b + 1))
                sp.dma_start(v_parts[b].rearrange("h p c -> p h c"), v_sb[:, :, :, :].rearrange("p h k c -> p h (k c)"))\
                  .then_inc(v_saved, 16)
                sp.wait_ge(bank_drained[GT_JOB[0]], use(GT_JOB, b))
                sp.wait_ge(bank_drained[G_JOB[-1][0]], use(G_JOB[-1], b))
                sp.dma_start(u_parts[b], u_sb[:, 1, :]).then_inc(u_saved, 16)

            def next_batch(b):
                sp.wait_ge(bank_filled[XT_JOB[-1][0]], use(XT_JOB[-1], b))
                sp.dma_start(x_sb[:, 0], x_in[b + 1]).then_inc(x_loaded, 16)
                sp.wait_ge(bank_filled[CT_JOB[-1][0]], use(CT_JOB[-1], b))
                sp.dma_start(ctx_sb, ctx_in[b + 1]).then_inc(ctx_loaded, 16)
                store_batch(b)

            sp.wait_ge(row_max_ready, 1)
            next_batch(0)
            with sp.Fori(1, B - 1) as b:
                next_batch(b)

            def load_u(b, par):
                sp.dma_start(u_sb[:, par, :], u_parts[b]).then_inc(u_loaded, 16)

            def load_heads(b, i, blk, free):
                for r in range(RING):
                    rows = bass.ds(i * (RING * D) + r * D, D)
                    if free:
                        sp.wait_ge(scores_filled, BLK * blk + ST * (r + 1) - BLK)
                    for a0, n in ((0, 3), (3, 2), (5, 1)):
                        sp.dma_start(q_ring[a0 * D:(a0 + n) * D, r, :], q_parts[b, 0:n, rows, :])\
                          .then_inc(head_loaded[r], 16)
                    if free:
                        sp.wait_ge(out_filled, BLK // 2 * blk + ST // 2 * (r + 1) - BLK // 2)
                    sp.dma_start(v_ring[:, r].rearrange("p k c -> p (k c)"), v_parts[b, bass.ds(i * RING + r, 1), :, :]
                                 .rearrange("a p c -> p (a c)")).then_inc(head_loaded[r], 16)
                    for kp, (a0, n) in enumerate(((0, 3), (3, 2), (5, 1))):
                        sp.dma_start(k_ring[a0 * D:(a0 + n) * D, r, :],
                                     k_parts[b, kp, rows, :].unsqueeze(0).broadcast_to([n, D, T])).then_inc(head_loaded[r], 16)

            sp.wait_ge(u_saved, 1 + 16)
            load_u(0, 0)
            sp.wait_ge(parts_saved, 1 + 16 * 2 * NC)
            sp.wait_ge(v_saved, 1 + 16)
            load_heads(0, 0, 0, False)
            store_batch(B - 1)
            sp.wait_ge(parts_saved, 1 + 16 * 2 * NC * B)
            sp.wait_ge(v_saved, 1 + 16 * B)
            sp.wait_ge(u_saved, 1 + 16 * B)
            with sp.Fori(1, BLOCKS) as i:
                load_heads(0, i, i, True)
            load_u(1, 1)
            with sp.Fori(0, BLOCKS) as i:
                load_heads(1, i, BLOCKS + i, True)
            with sp.Fori(1, B // 2) as pair:
                for par in range(2):
                    sp.wait_ge(quad_filled, H * ST * (2 * pair + par - 1))
                    apart(sp)
                    load_u(2 * pair + par, par)
                    with sp.Fori(0, BLOCKS) as i:
                        load_heads(2 * pair + par, i, BLOCKS * (2 * pair + par) + i, True)

            def load_x(b, par):
                sp.dma_start(x_sb[:, par], x_in[b]).then_inc(x_reloaded[par], 16)

            out_v = out.rearrange("b (s p) c -> b p s c", p=P)

            def store_y(b):
                for s in range(ST):
                    sp.wait_ge(y_ready, ST * b + s + 1)
                    sp.dma_start(out_v[b, :, s, :], y_sb[:, s, :]).then_inc(y_stored, 16)

            sp.wait_ge(bank_filled[XT_JOB[-1][0]], use(XT_JOB[-1], B - 1))
            load_x(0, 0)
            load_x(1, 1)
            with sp.Fori(0, B // 2 - 1) as pair:
                for par in range(2):
                    store_y(2 * pair + par)
                    load_x(2 * pair + par + 2, par)
            store_y(B - 2)
            store_y(B - 1)
            sp.wait_ge(y_stored, 16 * ST * B)

        @block.gpsimd
        def _(pool):
            nc.gpsimd.memset(ident[:, :], 0.0).then_inc(consts_made, 1)
            nc.gpsimd.memset(ident16[:, :], 0.0).then_inc(consts_made, 1)
            nc.gpsimd.memset(headmask[:, :, :], 1.0).then_inc(consts_made, 1)
            nc.gpsimd.memset(ones_row[:, :], 1.0).then_inc(consts_made, 1)
            nc.gpsimd.memset(ip_probs_t[:, :, :], 1.0).then_inc(consts_made, 1)
            nc.gpsimd.memset(v_sb[:, :, :, VCOLS - 1:VCOLS], 1.0).then_inc(consts_made, 1)
            nc.gpsimd.memset(row_max[:, :], 0.0).then_inc(consts_made, 1)
            nc.gpsimd.memset(wvx[:, :, :, C:C + N_IP], 0.0).then_inc(consts_made, 1)
            pool.wait_ge(consts_made, 8)
            nc.gpsimd.affine_select(out=ident[:, :], in_=ident[:, :], compare_op=ALU.not_equal, fill=1.0, base=0,
                                    pattern=[[-1, P]], channel_multiplier=1).then_inc(consts_made, 1)
            nc.gpsimd.affine_select(out=ident16[:, :], in_=ident16[:, :], compare_op=ALU.not_equal, fill=1.0, base=0,
                                    pattern=[[-1, P]], channel_multiplier=1).then_inc(consts_made, 1)
            nc.gpsimd.affine_select(out=headmask[:, :, :], in_=headmask[:, :, :], compare_op=ALU.is_ge, fill=0.0,
                                    base=0, pattern=[[P, NC], [-D, H]], channel_multiplier=1).then_inc(consts_made, 1)
            pool.wait_ge(consts_made, 11)
            nc.gpsimd.affine_select(out=headmask[:, :, :], in_=headmask[:, :, :], compare_op=ALU.is_ge, fill=0.0,
                                    base=D - 1, pattern=[[-P, NC], [D, H]], channel_multiplier=-1)\
              .then_inc(consts_made, 1)

            def block_diagonal(bd, src):
                for m, (c0, cn) in enumerate(CT):
                    tokens = src[0:cn, m, :].rearrange("p (b n) -> p b n", b=B)
                    last = nc.gpsimd.tensor_tensor(
                        bd[0:cn, m].rearrange("p b (h n) -> p b h n", n=N_IP), tokens.unsqueeze(2).broadcast_to([cn, B, H, N_IP]),
                        headmask[0:cn, m, :].unsqueeze(1).unsqueeze(3).broadcast_to([cn, B, H, N_IP]), ALU.mult)
                return last

            pool.sem_inc(parts_split, R1)
            pool.sem_inc(head_reduced, 2)
            pool.sem_inc(weight_ready, 2)
            for saved in (parts_saved, v_saved, u_saved):
                pool.sem_inc(saved, 1)

            def batch(b, first):
                for t in range(2 * NC):
                    cn = CT[t % NC][1]
                    n = S if t < NC else T
                    pool.wait_ge(mid_split, 2 * NC * b + t + 1)
                    nc.gpsimd.tensor_tensor(parts[0:cn, t, 2, 0:n], resid[0:cn, t % R1, 0:n], parts[0:cn, t, 1, 0:n],
                                            ALU.subtract).then_inc(parts_split, 1)
                if first:
                    pool.wait_ge(bank_drained[2], ip_use(2))
                else:
                    pool.wait_ge(bank_filled[IPS_JOB[0]], use(IPS_JOB, b - 1))
                apart(pool)
                for m, (c0, cn) in enumerate(CT):
                    last = nc.gpsimd.tensor_copy(kip_batch[0:cn, m, :], kip_bd[0:cn, m, b, :])
                last.then_inc(kip_ready, 1)
                pool.wait_ge(bank_drained[V_JOB[-1][0]], use(V_JOB[-1], b))
                apart(pool)
                for a in range(2):
                    nc.gpsimd.tensor_copy(v_sb[:, :, :, a * VW_PART + D:(a + 1) * VW_PART],
                                          sem_parts[:, a].unsqueeze(1).broadcast_to([TP, H, TT, N_IP])).then_inc(sem_step, 1)

            batch(0, True)
            with pool.Fori(1, B) as b:
                batch(b, False)
            pool.wait_ge(bank_filled[IPS_JOB[0]], use(IPS_JOB, B - 1))
            pool.wait_ge(parts_split, R1 + 2 * NC * B)
            block_diagonal(vip_bd, vip).then_inc(vip_bd_ready, 1)

            def weigh(v, st):
                pool.wait_ge(half_ready, v + 1)
                pool.wait_ge(norms_done, v + 1)
                nc.gpsimd.tensor_tensor(weight[:, st % 2, :], probs[:, st, :], half_hi[:, st % 2, :], ALU.subtract)\
                  .then_inc(weight_ready, 1)

            def reduce_head(g, slot):
                pool.wait_ge(out_drained, 2 + 2 * g + 2)
                apart(pool)
                raw = out_raw[:, 2 * slot:2 * slot + 2].rearrange("p a u c -> p (a u) c")
                nc.gpsimd.tensor_copy(reduced[:, g, :, VW_PART:RCOLS], raw[:, :, VCOLS - 1:VCOLS])
                nc.gpsimd.tensor_tensor(reduced[:, g, :, 0:VW_PART], raw[:, :, 0:VW_PART],
                                        raw[:, :, VW_PART:2 * VW_PART], ALU.add).then_inc(head_reduced, 1)

            def head_steps(g, slot, first):
                for j in range(ST):
                    weigh(ST * g + j, j)
                    if j == ST - 1 and not first:
                        reduce_head(g - 1, (slot - 1) % 2)

            head_steps(0, 0, True)
            head_steps(1, 1, False)
            with pool.Fori(1, HEADS // 2) as g2:
                for slot in range(2):
                    head_steps(2 * g2 + slot, slot, False)
            reduce_head(HEADS - 1, 1)

            pool.wait_ge(head_reduced, 2 + HEADS)

            def step(b, par, free):
                if free:
                    pool.wait_ge(text_t_filled, (NC + 1) * (b - 1))
                    apart(pool)
                    apart(pool)
                pool.wait_ge(inv_sum_ready, b + 1)
                apart(pool)
                red_b = reduced[:, bass.ds(b * H, H), :, 0:D]
                inv_b = inv_sum[:, par, :].rearrange("p (h s) -> p h s", s=ST)
                nc.gpsimd.tensor_tensor(text[:, par].rearrange("p s (h d) -> p h s d", d=D), red_b,
                                        inv_b.unsqueeze(3).broadcast_to([P, H, ST, D]), ALU.mult)\
                  .then_inc(text_ready, 1)

            step(0, 0, False)
            step(1, 1, False)
            with pool.Fori(1, B // 2) as pair:
                for par in range(2):
                    step(2 * pair + par, par, True)

        @block.scalar
        def _(act):
            act.dma_start(wq_raw[:, 0:2, :], w_q[0:2 * P, :].rearrange("(m p) c -> p m c", p=P)).then_inc(wq_loaded, 16)
            act.dma_start(wq_raw[0:CT[2][1], 2, :], w_q[2 * P:C, :]).then_inc(wq_loaded, 16)
            act.dma_start(wk_raw, w_k.rearrange("(e p) c -> p e c", p=P)).then_inc(wk_loaded, 16)
            act.dma_start(wv_raw, w_v.rearrange("(e p) c -> p e c", p=P)).then_inc(wv_loaded, 16)
            act.dma_start(wout[:, 0:2, :], w_out[0:2 * P, :].rearrange("(m p) c -> p m c", p=P)).then_inc(wout_loaded, 16)
            act.dma_start(wout[0:CT[2][1], 2, :], w_out[2 * P:C, :]).then_inc(wout_loaded, 16)
            act.dma_start(mask_col[:, :], spatial_mask.rearrange("(s p) -> p s", p=P), allow_slow_non_contiguous=True).then_inc(late_loaded, 16)
            for b in range(B):
                act.dma_start(vw[HIP:HIP + 1, b, :], b_out.rearrange("(a c) -> a c", a=1)).then_inc(late_loaded, 16)

            def scale_root(b):
                act.wait_ge(top_ready, b + 1)
                nc.scalar.activation(top[:, 1, :], top[:, 0, :], ACT.Sqrt, scale=IN_TOP ** -2).then_inc(top_root_ready, 1)

            act.wait_ge(w_top_ready, 1)
            nc.scalar.activation(w_top[:, 1, :], w_top[:, 0, :], ACT.Sqrt, scale=IN_TOP ** -2).then_inc(w_root_ready, 1)
            scale_root(0)
            act.wait_ge(ip_step, 1)
            nc.scalar.activation(ip_stat[:, 1:2], ip_stat[:, 0:1], ACT.Sqrt).then_inc(ip_root, 1)
            act.wait_ge(wq_padded, 1)
            act.wait_ge(bank_drained[W_SCALE[0]], use(W_SCALE, 0))

            def weight_first(w, raw, n):
                nc.scalar.activation(w[:, 0, :, 0:C], raw, ACT.Identity, scale=w_scale[:, n:n + 1]).then_inc(w_hi_split, 1)

            weight_first(wq, wq_raw, 2)

            def ip_tokens():
                act.wait_ge(bank_filled[0], ip_use(0))
                nc.scalar.activation(ip_t, bank[0][:, 0:ET * ALLIP].rearrange("p (e i) -> p e i", e=ET), ACT.Copy)\
                  .then_inc(bank_drained[0], 1)
                act.wait_ge(bank_filled[1], ip_use(1))
                nc.scalar.activation(ipn_t[:, 0], bank[1][:, 0:ET * ALLIP].rearrange("p (e i) -> p e i", e=ET),
                                     ACT.Copy, scale=IN_TOP).then_inc(ipn_hi_split, 1)
                act.wait_ge(bank_drained[1], ip_use(1))

            def batch(b, first, last):
                act.wait_ge(bank_drained[SCALE_JOB[0]], use(SCALE_0, 0) if first else use(SCALE_JOB, b - 1))
                apart(act)
                for t in range(IN_TILES):
                    j = (XT_JOB + CT_JOB)[t]
                    act.wait_ge(bank_filled[j[0]], use(j, b))
                    if t < NC:
                        cn = CT[t][1]
                        nc.scalar.activation(x_t[0:cn, 0, t, :], bank[j[0]][0:cn, 0:S], ACT.Identity,
                                             scale=scale[0:cn, X_COL:X_COL + 1]).then_inc(in_hi_split, 1)
                    else:
                        nc.scalar.activation(ctx_t[:, 0, t - NC, :], bank[j[0]][:, 0:T], ACT.Identity,
                                             scale=scale[:, CTX_COL:CTX_COL + 1]).then_inc(in_hi_split, 1)
                if first:
                    weight_first(wk, wk_raw, 0)
                    weight_first(wvx, wv_raw, 1)

                def ip_columns():
                    nc.scalar.activation(wvx[:, :, :, C:C + N_IP].rearrange("p a e c -> p (a e) c"),
                                         ipn_t[:, :, :, bass.ds(b * N_IP, N_IP)].rearrange("p a e c -> p (a e) c"), ACT.Copy)\
                      .then_inc(ip_cols_ready, 1)

                if not first:
                    ip_columns()

                def middle(t):
                    j, cn = (Q_JOB + K_JOB)[t], CT[t % NC][1]
                    n = S if t < NC else T
                    act.wait_ge(bank_drained[j[0]], use(j, b))
                    nc.scalar.activation(parts[0:cn, t, 1, 0:n], resid[0:cn, t % R1, 0:n], ACT.Copy).then_inc(mid_split, 1)

                act.wait_ge(parts_saved, 1 + 16 * 2 * NC * b)
                for t in range(2 * NC):
                    j, c0, cn = (Q_JOB + K_JOB)[t], *CT[t % NC]
                    act.wait_ge(bank_filled[j[0]], use(j, b))
                    if t < NC:
                        nc.scalar.activation(q_full[0:cn, t, :], bank[j[0]][0:cn, 0:S], ACT.Identity,
                                             scale=scale[0:cn, Q_COL:Q_COL + 1]).then_inc(q_full_ready, 1)
                        nc.scalar.activation(parts[0:cn, t, 0, 0:S], bank[j[0]][0:cn, 0:S], ACT.Identity,
                                             scale=scale[0:cn, Q_COL:Q_COL + 1]).then_inc(hi_split, 1)
                    else:
                        nc.scalar.activation(parts[0:cn, t, 0, 0:T], bank[j[0]][0:cn, 0:T], ACT.Identity,
                                             scale=scale[0:cn, K_COL:K_COL + 1]).then_inc(hi_split, 1)
                    if t > 0:
                        middle(t - 1)
                if first:
                    ip_tokens()
                    ip_columns()
                act.wait_ge(v_saved, 1 + 16 * b)
                for k in range(TT):
                    j = V_JOB[k]
                    v_k = v_sb[:, :, k, :]
                    act.wait_ge(bank_filled[j[0]], use(j, b))
                    nc.scalar.activation(v_k[:, :, 0:D], bank[j[0]][0:TP, 0:C].rearrange("p (h d) -> p h d", d=D), ACT.Copy,
                                         scale=V_DOWN)
                    nc.scalar.activation(sem_parts[:, 0, k, :], bank[j[0]][0:TP, C:C + N_IP], ACT.Copy,
                                         scale=SEM_DOWN).then_inc(v_hi_split, 1)
                    if k == 0:
                        middle(2 * NC - 1)
                act.wait_ge(bank_filled[IPS_JOB[0]], use(IPS_JOB, b))
                apart(act)
                nc.scalar.activation(ip_scores[:, b].rearrange("p h s n -> p s h n"),
                                     bank[IPS_JOB[0]][:, 0:ST * HIP].rearrange("p (s h n) -> p s h n", s=ST, n=N_IP), ACT.Copy)\
                  .then_inc(bank_drained[IPS_JOB[0]], 1)
                act.wait_ge(u_saved, 1 + 16 * b)
                for k in range(TT):
                    j, n = G_JOB[k], U_COLS[k]
                    act.wait_ge(bank_filled[j[0]], use(j, b))
                    nc.scalar.activation(u_sb[:, 1, GH[k] + k * TP:GH[k] + T], bank[j[0]][0:TP, 0:n], ACT.Copy,
                                         scale=GRAM_SCALE).then_inc(gram_hi_split, 1)
                    if n > TP:
                        if k >= 2:
                            act.wait_ge(bank_drained[G_JOB[k - 2][0]], use(G_JOB[k - 2], b))
                        nc.scalar.activation(gram_hi2[:, k % 2, 0:n - TP], bank[j[0]][0:TP, TP:n], ACT.Copy,
                                             scale=2.0 * GRAM_SCALE).then_inc(gram_hi2_split, 1)
                    if k == 0 and not last:
                        scale_root(b + 1)
                act.wait_ge(bank_filled[GT_JOB[0]], use(GT_JOB, b))
                for k in range(1, TT):
                    src = bank16(GT_JOB[0])[0:TP, GT_COL[k]:GT_COL[k] + k * P].rearrange("p (i t) -> p i t", t=P)[:, :, 0:TP]
                    last_copy = nc.scalar.activation(u_sb[:, 1, GH[k]:GH[k] + k * TP].rearrange("p (i t) -> p i t", t=TP), src, ACT.Copy)
                last_copy.then_inc(bank_drained[GT_JOB[0]], 1)

            batch(0, True, False)
            with act.Fori(1, B - 1) as b:
                batch(b, False, False)
            batch(B - 1, False, True)

            def exp(v, st, free):
                act.wait_ge(row_max_found, v + 1)
                if free:
                    act.wait_ge(norms_done, v - 1)
                nc.scalar.activation(probs[:, st, :], bank[S_BANK + st % 2][:, 0:T], ACT.Exp, bias=neg_max[:, st:st + 1])\
                  .then_inc(probs_ready, 1)

            def halve(v, st):
                act.wait_ge(probs_ready, v + 1)
                act.wait_ge(weight_ready, v + 1)
                nc.scalar.activation(half_hi[:, st % 2, :], probs[:, st, :], ACT.Copy, scale=0.5).then_inc(half_ready, 1)

            def hi(v, par):
                act.wait_ge(probs_t_filled, v + 1)
                nc.scalar.activation(probs_hi[:, par, :], bank[PT_BANK + par][0:TP, 0:S], ACT.Copy, scale=PROB_SCALE)\
                  .then_inc(hi_ready, 1)

            def drain_out(g, pair, slot):
                act.wait_ge(out_filled, 2 * g + pair + 1)
                act.wait_ge(head_reduced, g + 1)
                nc.scalar.activation(out_raw[:, 2 * slot + pair].rearrange("p u c -> p (u c)"),
                                     bank[O_BANK + pair][:, 0:2 * VCOLS], ACT.Copy).then_inc(out_drained, 1)

            def head_steps(g, slot, first):
                for j in range(ST):
                    if not (first and j < 2):
                        hi(ST * g + j - 1, (j - 1) % 2)
                    exp(ST * g + j, j, not first)
                    if first and j == 1:
                        hi(0, 0)
                    halve(ST * g + j, j)
                    if j % 2 == 0 and not first:
                        drain_out(g - 1, j // 2, (slot - 1) % 2)

            head_steps(0, 0, True)
            head_steps(1, 1, False)
            with act.Fori(1, HEADS // 2) as g2:
                for slot in range(2):
                    head_steps(2 * g2 + slot, slot, False)
            hi(UNITS - 1, (ST - 1) % 2)
            for pair in range(2):
                drain_out(HEADS - 1, pair, 1)

            act.wait_ge(square_ready, 1)
            nc.scalar.activation(root, square, ACT.Sqrt).then_inc(root_ready, 1)

            def ip_exps(b):
                act.wait_ge(ip_fused, b + 1)
                nc.scalar.activation(ip_exp, fused, ACT.Exp, scale=SEM_SCALE).then_inc(ip_exp_ready, 1)

            def step(b, par):
                for c, (c0, cn) in enumerate(CT):
                    act.wait_ge(text_t_filled, (NC + 1) * b + c + 1)
                    nc.scalar.activation(text_t[0:cn, par, c, :], bank[c][0:cn, 0:S], ACT.Copy).then_inc(text_t_ready, 1)
                act.wait_ge(text_t_filled, (NC + 1) * b + NC + 1)
                nc.scalar.activation(ip_probs_t[0:HIP, par, :], bank[NC][0:HIP, 0:S], ACT.Copy).then_inc(text_t_ready, 1)

            ip_exps(0)
            for b in range(B):
                act.wait_ge(vw_filled, b + 1)
                nc.scalar.activation(vw[0:HIP, b, :], bank[b][0:HIP, 0:C], ACT.Copy).then_inc(vw_ready, 1)
            step(0, 0)
            ip_exps(1)
            step(1, 1)
            with act.Fori(1, B // 2) as pair:
                for par in range(2):
                    ip_exps(2 * pair + par)
                    step(2 * pair + par, par)

        @block.vector
        def _(dve):
            dve.sem_inc(norms_done, 2)
            dve.sem_inc(out_drained, 2)
            def squares(b):
                for n_done, k in enumerate([*range(TT, TT + ST), *range(TT)]):
                    if k == 0:
                        dve.wait_ge(ctx_loaded, 16 * (b + 1))
                    if k == TT:
                        dve.wait_ge(x_loaded, 16 * (b + 1))
                    if n_done >= 2:
                        dve.wait_ge(sumsq_ready, (TT + ST) * b + n_done - 1)
                    a, n, pn = (ctx_sb[:, k, :], E, TP) if k < TT else (x_sb[:, 0, k - TT, :], C, P)
                    nc.vector.scalar_tensor_tensor(discard[0:pn, k % 2, 0:n], a, 1.0, a, ALU.mult, ALU.mult,
                                                   accum_out=sumsq[0:pn, k:k + 1]).then_inc(sumsq_ready, 1)
                dve.wait_ge(sumsq_ready, (TT + ST) * (b + 1))
                nc.vector.tensor_reduce(row_max[0:TP, 0:1], sumsq[0:TP, 0:TT], AX.X, ALU.max)
                nc.vector.tensor_reduce(row_max[:, 1:2], sumsq[:, TT:TT + ST], AX.X, ALU.max).then_inc(row_max_ready, 1)

            def find_top(job, job_b, b):
                dve.wait_ge(bank_filled[job[0]], use(job, job_b))
                nc.vector.tensor_reduce(top[:, 0, :], bank[job[0]][0:1, 0:2 * P].rearrange("p (a t) -> p a t", a=2), AX.X, ALU.max)\
                  .then_inc(bank_drained[job[0]], 1)
                dve.wait_ge(bank_drained[job[0]], use(job, job_b))
                nc.vector.tensor_scalar(top[:, 0, :], top[:, 0, :], TINY, None, ALU.max).then_inc(top_ready, 1)

            def make_scales(b):
                dve.wait_ge(top_root_ready, b + 1)
                bound = top[:, 1, :]
                nc.vector.reciprocal(scale_row[:, CTX_COL:X_COL + 1], bound).then_inc(scale_row_ready, 1)
                nc.vector.tensor_scalar(scale_row[:, K_COL:K_COL + 2], w_top[:, 2, 0:2], bound[:, 0:1], None, ALU.mult)\
                  .then_inc(scale_row_ready, 1)
                nc.vector.tensor_scalar(scale_row[:, Q_COL:Q_COL + 1], w_top[:, 1, 2:3], bound[:, 1:2], None, ALU.mult)\
                  .then_inc(scale_row_ready, 1)

            def spread_scales(job, job_b, b):
                dve.wait_ge(bank_filled[job[0]], use(job, job_b))
                nc.vector.tensor_copy(kept_scale[:, b, 0:1], bank[job[0]][:, 4:5])
                nc.vector.tensor_copy(kept_scale[:, b, 1:2], bank[job[0]][:, CTX_COL:CTX_COL + 1])
                nc.vector.tensor_copy(scale[:, :], bank[job[0]][:, 0:4]).then_inc(bank_drained[job[0]], 1)

            nc.vector.memset(wq_raw[CT[-1][1]:P, NC - 1, :], 0.0).then_inc(wq_padded, 1)
            dve.wait_ge(consts_made, CONSTS)
            squares(0)
            dve.wait_ge(wq_padded, 1)
            for n, raw, loaded, count in ((2, wq_raw, wq_loaded, 32), (0, wk_raw, wk_loaded, 16), (1, wv_raw, wv_loaded, 16)):
                dve.wait_ge(loaded, count)
                nc.vector.scalar_tensor_tensor(w_squares[n][:, 0:raw.shape[1], :], raw, 1.0, raw, ALU.mult, ALU.mult,
                                               accum_out=w_sums[:, n:n + 1]).then_inc(w_sums_ready, 1)
            dve.wait_ge(ip_loaded, 16 * B)
            nc.vector.scalar_tensor_tensor(ip_squares, ip_rows[:, 0, :], 1.0, ip_rows[:, 0, :], ALU.mult, ALU.mult,
                                           accum_out=ip_stat[:, 0:1]).then_inc(ip_step, 1)
            dve.wait_ge(bank_filled[W_TOP[0]], use(W_TOP, 0))
            nc.vector.tensor_reduce(w_top[:, 0, :], bank[W_TOP[0]][0:1, 0:3 * P].rearrange("p (a t) -> p a t", a=3), AX.X, ALU.max)\
              .then_inc(bank_drained[W_TOP[0]], 1)
            dve.wait_ge(bank_drained[W_TOP[0]], use(W_TOP, 0))
            nc.vector.tensor_scalar(w_top[:, 0, :], w_top[:, 0, :], TINY, None, ALU.max).then_inc(w_top_ready, 1)
            find_top(TOP_0, 0, 0)
            dve.wait_ge(w_root_ready, 1)
            nc.vector.reciprocal(w_row[:, :], w_top[:, 1, :]).then_inc(w_row_ready, 1)
            nc.vector.tensor_scalar(w_top[:, 2, 0:1], w_top[:, 1, 0:1], SCALE, None, ALU.mult).then_inc(w_row_ready, 1)
            nc.vector.tensor_scalar(w_top[:, 2, 1:2], w_top[:, 1, 1:2], 1.0 / V_DOWN, None, ALU.mult).then_inc(w_row_ready, 1)
            dve.wait_ge(w_row_ready, 3)
            make_scales(0)
            dve.wait_ge(bank_filled[W_SCALE[0]], use(W_SCALE, 0))
            nc.vector.tensor_copy(w_scale[:, :], bank[W_SCALE[0]][:, 0:3]).then_inc(bank_drained[W_SCALE[0]], 1)
            spread_scales(SCALE_0, 0, 0)

            def weight_rest(w, raw, col, nth):
                dve.wait_ge(w_hi_split, nth)
                nc.vector.scalar_tensor_tensor(w[:, 1, :, 0:C], raw, w_scale[:, col:col + 1], w[:, 0, :, 0:C], ALU.mult,
                                               ALU.subtract).then_inc(w_split, 1)

            weight_rest(wq, wq_raw, 2, 1)

            def ip_norms():
                dve.wait_ge(ip_root, 1)
                nc.vector.tensor_scalar(ip_stat[:, 2:3], ip_stat[:, 1:2], 1e-18, None, ALU.max).then_inc(ip_step, 1)
                dve.wait_ge(ip_step, 2)
                nc.vector.reciprocal(ip_stat[:, 3:4], ip_stat[:, 2:3]).then_inc(ip_step, 1)
                dve.wait_ge(ip_step, 3)
                nc.vector.scalar_tensor_tensor(ip_stat[:, 4:5], ip_stat[:, 0:1], ip_stat[:, 3:4], ip_stat[:, 2:3], ALU.mult,
                                               ALU.add).then_inc(ip_step, 1)
                dve.wait_ge(ip_step, 4)
                nc.vector.tensor_scalar(ip_stat[:, 5:6], ip_stat[:, 4:5], 0.5, EPS, ALU.mult, ALU.max).then_inc(ip_step, 1)
                dve.wait_ge(ip_step, 5)
                nc.vector.reciprocal(ip_stat[:, 6:7], ip_stat[:, 5:6]).then_inc(ip_step, 1)
                dve.wait_ge(ip_step, 6)
                nc.vector.tensor_scalar(ip_rows[:, 1, :], ip_rows[:, 0, :], ip_stat[:, 6:7], None, ALU.mult).then_inc(ip_step, 1)

            def ip_tokens():
                dve.wait_ge(ipn_hi_split, 1)
                nc.vector.scalar_tensor_tensor(ipn_t[:, 1], bank[1][:, 0:ET * ALLIP].rearrange("p (e i) -> p e i", e=ET), IN_TOP,
                                               ipn_t[:, 0], ALU.mult, ALU.subtract).then_inc(bank_drained[1], 1)
                dve.wait_ge(bank_filled[2], ip_use(2))
                for m, (c0, cn) in enumerate(CT):
                    src = bank[2][0:cn, m * ALLIP:(m + 1) * ALLIP].rearrange("p (b n) -> p b n", b=B)
                    last = nc.vector.tensor_tensor(
                        kip_bd[0:cn, m].rearrange("p b (h n) -> p b h n", n=N_IP),
                        src.unsqueeze(2).broadcast_to([cn, B, H, N_IP]),
                        headmask[0:cn, m, :].unsqueeze(1).unsqueeze(3).broadcast_to([cn, B, H, N_IP]), ALU.mult)
                last.then_inc(bank_drained[2], 1)
                dve.wait_ge(bank_filled[3], ip_use(3))
                for m, (c0, cn) in enumerate(CT):
                    last = nc.vector.tensor_copy(vip[0:cn, m, :], bank[3][0:cn, m * ALLIP:(m + 1) * ALLIP])
                last.then_inc(bank_drained[3], 1)

            def batch(b, first, last):
                for t in range(IN_TILES):
                    j = (XT_JOB + CT_JOB)[t]
                    dve.wait_ge(in_hi_split, IN_TILES * b + t + 1)
                    if t < NC:
                        cn = CT[t][1]
                        nc.vector.scalar_tensor_tensor(x_t[0:cn, 1, t, :], bank[j[0]][0:cn, 0:S], scale[0:cn, X_COL:X_COL + 1],
                                                       x_t[0:cn, 0, t, :], ALU.mult, ALU.subtract).then_inc(bank_drained[j[0]], 1)
                    else:
                        nc.vector.scalar_tensor_tensor(ctx_t[:, 1, t - NC, :], bank[j[0]][:, 0:T], scale[:, CTX_COL:CTX_COL + 1],
                                                       ctx_t[:, 0, t - NC, :], ALU.mult, ALU.subtract).then_inc(bank_drained[j[0]], 1)
                if first:
                    weight_rest(wk, wk_raw, 0, 2)
                    ip_norms()
                    weight_rest(wvx, wv_raw, 1, 3)

                def residual(t):
                    j, c0, cn = (Q_JOB + K_JOB)[t], *CT[t % NC]
                    n, col = (S, Q_COL) if t < NC else (T, K_COL)
                    dve.wait_ge(hi_split, 2 * NC * b + t + 1)
                    dve.wait_ge(parts_split, 2 * NC * b + t + 1)
                    nc.vector.scalar_tensor_tensor(resid[0:cn, t % R1, 0:n], bank[j[0]][0:cn, 0:n], scale[0:cn, col:col + 1],
                                                   parts[0:cn, t, 0, 0:n], ALU.mult, ALU.subtract)\
                      .then_inc(bank_drained[j[0]], 1)

                for t in range(NC):
                    residual(t)
                for t in range(NC, 2 * NC):
                    residual(t)
                if first:
                    ip_tokens()
                for k in range(TT):
                    j = V_JOB[k]
                    v_k = v_sb[:, :, k, :]
                    dve.wait_ge(v_hi_split, TT * b + k + 1)
                    nc.vector.scalar_tensor_tensor(v_k[:, :, VW_PART:VW_PART + D],
                                                   bank[j[0]][0:TP, 0:C].rearrange("p (h d) -> p h d", d=D), V_DOWN,
                                                   v_k[:, :, 0:D], ALU.mult, ALU.subtract)
                    nc.vector.scalar_tensor_tensor(sem_parts[:, 1, k, :], bank[j[0]][0:TP, C:C + N_IP], SEM_DOWN,
                                                   sem_parts[:, 0, k, :], ALU.mult, ALU.subtract).then_inc(bank_drained[j[0]], 1)
                    if k == 1 and not last:
                        squares(b + 1)

                def gram(k):
                    j, n = G_JOB[k], U_COLS[k]
                    full = bank[j[0]]
                    dve.wait_ge(gram_hi_split, TT * b + k + 1)
                    if n > TP:
                        dve.wait_ge(gram_hi2_split, (TT - 1) * b + k + 1)
                        nc.vector.scalar_tensor_tensor(u_sb[:, 1, UL[k] + TP:UL[k] + n], full[0:TP, TP:n], 2.0 * GRAM_SCALE,
                                                       gram_hi2[:, k % 2, 0:n - TP], ALU.mult, ALU.subtract)
                    nc.vector.scalar_tensor_tensor(u_sb[:, 1, UL[k]:UL[k] + TP], full[0:TP, 0:TP], GRAM_SCALE,
                                                   u_sb[:, 1, GH[k] + k * TP:GH[k] + (k + 1) * TP],
                                                   ALU.mult, ALU.subtract).then_inc(bank_drained[j[0]], 1)

                if last:
                    dve.wait_ge(bank_filled[TOP_JOB[0]], use(TOP_JOB, b))
                    dve.sem_inc(bank_drained[TOP_JOB[0]], 1)
                    gram(0)
                    dve.wait_ge(bank_filled[SCALE_JOB[0]], use(SCALE_JOB, b))
                    dve.sem_inc(bank_drained[SCALE_JOB[0]], 1)
                else:
                    find_top(TOP_JOB, b, b + 1)
                    make_scales(b + 1)
                    gram(0)
                    dve.wait_ge(bank_drained[V_JOB[-1][0]], use(V_JOB[-1], b))
                    spread_scales(SCALE_JOB, b, b + 1)
                for k in range(1, TT):
                    gram(k)

            batch(0, True, False)
            with dve.Fori(1, B - 1) as b:
                batch(b, False, False)
            batch(B - 1, False, True)

            def row_maximum(v, st):
                dve.wait_ge(scores_filled, v + 1)
                nc.vector.tensor_reduce(neg_max[:, st:st + 1], bank[S_BANK + st % 2][:, 0:T], AX.X, ALU.max, negate=True)\
                  .then_inc(row_max_found, 1)

            def norm(v, st):
                dve.wait_ge(quad_filled, v + 1)
                dve.wait_ge(weight_ready, 2 + v + 1)
                nc.vector.scalar_tensor_tensor(discard[:, st % 2, 0:T], bank[Y_BANK + st % 2][:, 0:T], 1.0, weight[:, st % 2, :], ALU.mult,
                                               ALU.mult, accum_out=norms[:, bass.ds(v, 1)]).then_inc(norms_done, 1)

            def lo(v, par):
                dve.wait_ge(hi_ready, v + 1)
                nc.vector.scalar_tensor_tensor(probs_lo[:, par, :], bank[PT_BANK + par][0:TP, 0:S], PROB_SCALE,
                                               probs_hi[:, par, :], ALU.mult, ALU.subtract).then_inc(lo_ready, 1)

            def head_steps(g, first):
                for j in range(ST):
                    row_maximum(ST * g + j, j)
                    if not (first and j < 3):
                        norm(ST * g + j - 3, (j - 3) % ST)
                    if not (first and j == 0):
                        lo(ST * g + j - 1, (j - 1) % 2)

            head_steps(0, True)
            with dve.Fori(1, HEADS) as g:
                head_steps(g, False)
            norm(UNITS - 3, (UNITS - 3) % ST)
            lo(UNITS - 1, (UNITS - 1) % 2)
            norm(UNITS - 2, (UNITS - 2) % ST)
            norm(UNITS - 1, (UNITS - 1) % ST)

            dve.wait_ge(head_reduced, 2 + HEADS)
            dve.wait_ge(norms_done, 2 + UNITS)
            nc.vector.tensor_scalar(square, norms[:, :], 0.0, SQUARE_SCALE, ALU.max, ALU.mult).then_inc(square_ready, 1)
            dve.wait_ge(late_loaded, 16 * (1 + B))
            dve.wait_ge(root_ready, 1)

            fused3 = fused.rearrange("p (u n) -> p u n", n=N_IP)
            exp3 = ip_exp.rearrange("p (u n) -> p u n", n=N_IP)
            stat, stat2 = ip_stat3[:, 0:U], ip_stat3[:, U:2 * U]

            def over_tokens(a):
                return a.unsqueeze(2).broadcast_to([P, U, N_IP])

            ELEM = 14

            def elem(b, par, free):
                step = ELEM * b
                done = [0]

                def then(ins):
                    ins.then_inc(elem_step, 1)
                    done[0] += 1
                    dve.wait_ge(elem_step, step + done[0])

                sums = reduced[:, bass.ds(b * H, H), :, RCOLS - 1].rearrange("p h s -> p (h s)")
                if free:
                    dve.wait_ge(text_ready, b - 1)
                    apart(dve)
                then(nc.vector.reciprocal(inv_sum[:, par, :], sums))
                nc.vector.tensor_scalar(inv_sum[:, par, :], inv_sum[:, par, :], kept_scale[:, b, 0:1], None, ALU.mult)\
                  .then_inc(inv_sum_ready, 1)
                guard, inv_guard, ratio, twice, least, norm_b, inv_norm = norm_tmp
                root_b, square_b = root[:, bass.ds(b * U, U)], square[:, bass.ds(b * U, U)]
                then(nc.vector.tensor_scalar(guard, root_b, 1e-18, None, ALU.max))
                then(nc.vector.reciprocal(inv_guard, guard))
                then(nc.vector.tensor_tensor(ratio, square_b, inv_guard, ALU.mult))
                then(nc.vector.tensor_tensor(twice, ratio, guard, ALU.add))
                then(nc.vector.tensor_scalar(least, sums, kept_scale[:, b, 1:2], EPS * SEM_SCALED, ALU.mult, ALU.mult))
                then(nc.vector.scalar_tensor_tensor(norm_b, twice, 0.5, least, ALU.mult, ALU.max))
                then(nc.vector.reciprocal(inv_norm, norm_b))
                red_b = reduced[:, bass.ds(b * H, H), :, D:D + N_IP].rearrange("p h s n -> p (h s) n")
                then(nc.vector.tensor_tensor(fused3, red_b, over_tokens(inv_norm), ALU.mult))
                then(nc.vector.scalar_tensor_tensor(fused, ip_scores[:, b].rearrange("p h s n -> p (h s n)"), SCALE / SEM_SCALE,
                                                    fused, ALU.mult, ALU.add))
                then(nc.vector.tensor_reduce(stat, fused3, AX.X, ALU.max))
                nc.vector.tensor_tensor(fused3, fused3, over_tokens(stat), ALU.subtract).then_inc(ip_fused, 1)
                dve.wait_ge(ip_exp_ready, b + 1)
                then(nc.vector.tensor_reduce(stat, exp3, AX.X, ALU.add))
                then(nc.vector.reciprocal(stat2, stat))
                then(nc.vector.tensor_tensor(stat.rearrange("p (h s) -> p h s", s=ST), stat2.rearrange("p (h s) -> p h s", s=ST),
                                             mask_col[:, :].unsqueeze(1).broadcast_to([P, H, ST]), ALU.mult))
                assert done[0] == ELEM
                if free:
                    dve.wait_ge(text_t_filled, (NC + 1) * (b - 1))
                nc.vector.tensor_tensor(ip_probs[:, par].rearrange("p s (h n) -> p h s n", n=N_IP),
                                        exp3.rearrange("p (h s) n -> p h s n", s=ST),
                                        stat.rearrange("p (h s) -> p h s", s=ST).unsqueeze(3).broadcast_to([P, H, ST, N_IP]),
                                        ALU.mult).then_inc(ip_probs_ready, 1)

            def residual_add(b, half, par, free=True):
                dve.wait_ge(x_reloaded[par], 16 * (half + 1))
                for s in range(ST):
                    dve.wait_ge(y_filled, ST * b + s + 1)
                    if free:
                        dve.wait_ge(y_stored, 16 * ST * b)
                    nc.vector.tensor_tensor(y_sb[:, s, :], bank[4 + s][:, 0:C], x_sb[:, par, s, :], ALU.add)\
                      .then_inc(y_ready, 1)

            elem(0, 0, False)
            elem(1, 1, False)
            elem(2, 0, True)
            residual_add(0, 0, 0, False)
            elem(3, 1, True)
            residual_add(1, 0, 1)
            with dve.Fori(2, B // 2) as pair:
                elem(2 * pair, 0, True)
                residual_add(2 * pair - 2, pair - 1, 0)
                elem(2 * pair + 1, 1, True)
                residual_add(2 * pair - 1, pair - 1, 1)
            residual_add(B - 2, B // 2 - 1, 0)
            residual_add(B - 1, B // 2 - 1, 1)

        @block.tensor
        def _(pe):
            pe.wait_ge(consts_made, CONSTS)

            def row(job, cols, n, i):
                return nc.tensor.transpose(bank[job[0]][0:1, i * P:i * P + n], cols[0:n, i:i + 1], ident[0:n, 0:n])

            def tops(job, job_b, b):
                pe.wait_ge(row_max_ready, b + 1)
                row(job, row_max, P, 0)
                row(job, row_max, P, 1).then_inc(bank_filled[job[0]], 1)

            def scales(job, job_b, b):
                pe.wait_ge(bank_drained[job[0]], use(job, job_b) - 1)
                pe.wait_ge(scale_row_ready, 3 * (b + 1))
                nc.tensor.matmul(bank[job[0]][:, 0:5], ones_row[:, :], scale_row[:, :], start=True, stop=True)\
                  .then_inc(bank_filled[job[0]], 1)

            def first_scales():
                pe.wait_ge(w_sums_ready, 3)
                for i in range(3):
                    last = row(W_TOP, w_sums, P, i)
                last.then_inc(bank_filled[W_TOP[0]], 1)
                pe.wait_ge(bank_drained[W_TOP[0]], use(W_TOP, 0))
                tops(TOP_0, 0, 0)
                pe.wait_ge(bank_drained[TOP_0[0]], use(TOP_0, 0))
                pe.wait_ge(w_row_ready, 1)
                nc.tensor.matmul(bank[W_SCALE[0]][:, 0:3], ones_row[:, :], w_row[:, :], start=True, stop=True)\
                  .then_inc(bank_filled[W_SCALE[0]], 1)
                scales(SCALE_0, 0, 0)

            def ip_tokens():
                pe.wait_ge(bank_drained[0], ip_use(0) - 1)
                for e in range(ET):
                    last = nc.tensor.transpose(bank[0][:, e * ALLIP:(e + 1) * ALLIP], ip_rows[:, 0, e * P:(e + 1) * P],
                                               ident[0:ALLIP, 0:ALLIP])
                last.then_inc(bank_filled[0], 1)
                pe.wait_ge(ip_step, 7)
                pe.wait_ge(bank_drained[1], ip_use(1) - 1)
                for e in range(ET):
                    last = nc.tensor.transpose(bank[1][:, e * ALLIP:(e + 1) * ALLIP], ip_rows[:, 1, e * P:(e + 1) * P],
                                               ident[0:ALLIP, 0:ALLIP])
                last.then_inc(bank_filled[1], 1)
                pe.wait_ge(ip_weights_loaded, 32)
                pe.wait_ge(bank_drained[0], ip_use(0))
                for j, w in ((2, wk_ip), (3, wv_ip)):
                    pe.wait_ge(bank_drained[j], ip_use(j) - 1)
                    for m, (c0, cn) in enumerate(CT):
                        for e in range(ET):
                            last = nc.tensor.matmul(bank[j][0:cn, m * ALLIP:(m + 1) * ALLIP], w[:, e, c0:c0 + cn], ip_t[:, e, :],
                                                    start=(e == 0), stop=(e == ET - 1))
                    last.then_inc(bank_filled[j], 1)

            def batch(b, first, last_batch):
                def free(job):
                    count = use(job, b) - 1
                    if not isinstance(count, int) or count > 0:
                        pe.wait_ge(bank_drained[job[0]], count)

                def products(out, terms):
                    n = 0
                    for stationary, moving in terms:
                        for a, m in SPLIT:
                            n += 1
                            last = nc.tensor.matmul(out, stationary(a), moving(m), start=(n == 1), stop=(n == len(SPLIT) * len(terms)))
                    return last

                pe.wait_ge(x_loaded, 16 * (b + 1))
                for j in XT_JOB:
                    free(j)
                for c, (c0, cn) in enumerate(CT):
                    j = XT_JOB[c]
                    for s in range(ST):
                        last = nc.tensor.transpose(bank[j[0]][0:cn, s * P:(s + 1) * P], x_sb[:, 0, s, c0:c0 + cn], ident[:, :])
                    last.then_inc(bank_filled[j[0]], 1)
                pe.wait_ge(ctx_loaded, 16 * (b + 1))
                for e in range(ET):
                    j = CT_JOB[e]
                    free(j)
                    for k in range(TT):
                        last = nc.tensor.transpose(bank[j[0]][:, k * TP:(k + 1) * TP], ctx_sb[:, k, e * P:(e + 1) * P],
                                                   ident[0:TP, 0:TP])
                    last.then_inc(bank_filled[j[0]], 1)
                if first:
                    first_scales()
                    pe.wait_ge(w_split, 1)
                for m, (c0, cn) in enumerate(CT):
                    j = Q_JOB[m]
                    pe.wait_ge(bank_drained[XT_JOB[-1][0]], use(XT_JOB[-1], b))
                    free(j)
                    products(bank[j[0]][0:cn, 0:S],
                             [(lambda a, c=c, rn=rn: wq[0:rn, a, c, c0:c0 + cn], lambda a, c=c, rn=rn: x_t[0:rn, a, c, :])
                              for c, (r0, rn) in enumerate(CT)]).then_inc(bank_filled[j[0]], 1)
                if first:
                    pe.wait_ge(w_split, 2)
                pe.wait_ge(bank_drained[CT_JOB[-1][0]], use(CT_JOB[-1], b))
                for m, (c0, cn) in enumerate(CT):
                    j = K_JOB[m]
                    free(j)
                    products(bank[j[0]][0:cn, 0:T],
                             [(lambda a, e=e: wk[:, a, e, c0:c0 + cn], lambda a, e=e: ctx_t[:, a, e, :])
                              for e in range(ET)]).then_inc(bank_filled[j[0]], 1)
                if first:
                    ip_tokens()
                if first:
                    pe.wait_ge(w_split, 3)
                pe.wait_ge(ip_cols_ready, b + 1)
                for k in range(TT):
                    j = V_JOB[k]
                    free(j)
                    products(bank[j[0]][0:TP, 0:C + N_IP],
                             [(lambda a, e=e: ctx_t[:, a, e, k * TP:(k + 1) * TP], lambda a, e=e: wvx[:, a, e, :])
                              for e in range(ET)]).then_inc(bank_filled[j[0]], 1)
                free(IPS_JOB)
                pe.wait_ge(q_full_ready, NC * (b + 1))
                pe.wait_ge(kip_ready, b + 1)
                for s in range(ST):
                    for c, (r0, rn) in enumerate(CT):
                        h0, h1 = r0 // D * N_IP, (r0 + rn) // D * N_IP
                        last = nc.tensor.matmul(bank[IPS_JOB[0]][:, s * HIP + h0:s * HIP + h1], q_full[0:rn, c, s * P:(s + 1) * P],
                                                kip_batch[0:rn, c, h0:h1], start=True, stop=True)
                last.then_inc(bank_filled[IPS_JOB[0]], 1)
                def gram(k):
                    j = G_JOB[k]
                    free(j)
                    products(bank[j[0]][0:TP, 0:U_COLS[k]],
                             [(lambda a, e=e: ctx_t[:, a, e, k * TP:(k + 1) * TP], lambda a, e=e: ctx_t[:, a, e, k * TP:T])
                              for e in range(ET)]).then_inc(bank_filled[j[0]], 1)

                gram(0)
                free(TOP_JOB)
                if last_batch:
                    pe.sem_inc(bank_filled[TOP_JOB[0]], 1)
                else:
                    tops(TOP_JOB, b, b + 1)
                gram(1)
                if last_batch:
                    free(SCALE_JOB)
                    pe.sem_inc(bank_filled[SCALE_JOB[0]], 1)
                else:
                    scales(SCALE_JOB, b, b + 1)
                gram(2)
                gram(3)
                free(GT_JOB)
                pe.wait_ge(gram_hi_split, TT * b + TT - 1)
                for k in range(1, TT):
                    for i in range(k):
                        last = nc.tensor.transpose(bank16(GT_JOB[0])[0:TP, GT_COL[k] + i * P:GT_COL[k] + i * P + TP],
                                                   u_sb[:, 1, GH[i] + k * TP:GH[i] + (k + 1) * TP], ident16[0:TP, 0:TP])
                last.then_inc(bank_filled[GT_JOB[0]], 1)

            batch(0, True, False)
            with pe.Fori(1, B - 1) as b:
                batch(b, False, False)
            batch(B - 1, False, True)

            for j in range(8):
                pe.wait_ge(bank_drained[j], end_of_phase1(j))

            def scores(r, st, blk, u, free):
                if st == 0:
                    pe.wait_ge(head_loaded[r], 16 * 7 * (blk + 1))
                if free:
                    pe.wait_ge(probs_ready, u - 1)
                nc.tensor.matmul(bank[S_BANK + st % 2][:, 0:T], q_ring[:, r, st * P:(st + 1) * P], k_ring[:, r, :],
                                 start=True, stop=True).then_inc(scores_filled, 1)

            def transposes(st, u):
                pe.wait_ge(probs_ready, u + 1)
                for k in range(TT):
                    last = nc.tensor.transpose(bank[PT_BANK + st % 2][0:TP, k * P:(k + 1) * P],
                                               probs[:, st, k * TP:(k + 1) * TP], ident[:, :])
                last.then_inc(probs_t_filled, 1)

            def unit(j, u, blk, par, ahead):
                r, st = j // ST, j % ST
                y, o = bank[Y_BANK + st % 2][:, 0:T], bank[O_BANK + st // 2][:, (st % 2) * VCOLS:(st % 2 + 1) * VCOLS]

                if ahead > 1:
                    scores((j + 2) // ST % RING, (st + 2) % ST, blk + (j + 2) // BLK, u + 2, True)
                if ahead > 0:
                    transposes((st + 1) % ST, u + 1)
                pe.wait_ge(hi_ready, u + 1)
                pe.wait_ge(norms_done, u + 1)
                if st % 2 == 0:
                    pe.wait_ge(out_drained, BLK // 2 * blk + j // 2 + 1)
                for k in range(TT):
                    hi_k = probs_hi[:, st % 2, k * P:(k + 1) * P]
                    nc.tensor.matmul(o, hi_k, v_ring[:, r, k, :], start=(k == 0), stop=False)
                    nc.tensor.matmul(y, hi_k, u_sb[:, par, GH[k]:GH[k] + T], start=(k == 0), stop=False)
                    last = nc.tensor.matmul(y[:, k * TP:T], hi_k, u_sb[:, par, UL[k]:UL[k] + U_COLS[k]], start=False,
                                            stop=(k == TT - 1))
                last.then_inc(quad_filled, 1)
                pe.wait_ge(lo_ready, u + 1)
                for k in range(TT):
                    last = nc.tensor.matmul(o, probs_lo[:, st % 2, k * P:(k + 1) * P], v_ring[:, r, k, :], start=False,
                                            stop=(k == TT - 1))
                if st % 2 == 1:
                    last.then_inc(out_filled, 1)

            def heads(blk, par, last):
                for j in range(BLK):
                    unit(j, BLK * blk + j, blk, par, BLK - 1 - j if last else 2)

            scores(0, 0, 0, 0, False)
            scores(0, 1, 0, 1, False)
            transposes(0, 0)
            with pe.Fori(0, B // 2 - 1) as pair:
                for par in range(2):
                    pe.wait_ge(u_loaded, 16 * (2 * pair + par + 1))
                    apart(pe)
                    with pe.Fori(0, BLOCKS) as i:
                        heads(BLOCKS * (2 * pair + par) + i, par, False)
            pe.wait_ge(u_loaded, 16 * (B - 1))
            with pe.Fori(0, BLOCKS) as i:
                heads(BLOCKS * (B - 2) + i, 0, False)
            pe.wait_ge(u_loaded, 16 * B)
            with pe.Fori(0, BLOCKS - 1) as i:
                heads(BLOCKS * (B - 1) + i, 1, False)
            heads(BLOCKS * B - 1, 1, True)

            pe.wait_ge(wout_loaded, 32)
            pe.wait_ge(vip_bd_ready, 1)
            for b in range(B):
                if b == Y_BANK:
                    pe.wait_ge(norms_done, 2 + UNITS)
                    pe.wait_ge(out_drained, 2 + 2 * HEADS)
                for c, (r0, rn) in enumerate(CT):
                    last = nc.tensor.matmul(bank[b][0:HIP, 0:C], vip_bd[0:rn, c, b, :], wout[0:rn, c, :],
                                            start=(c == 0), stop=(c == NC - 1))
                last.then_inc(vw_filled, 1)

            def text_transposes(b, par, free):
                pe.wait_ge(text_ready, b + 1)
                if free:
                    pe.wait_ge(text_t_ready, (NC + 1) * b)
                for c, (c0, cn) in enumerate(CT):
                    for s in range(ST):
                        last = nc.tensor.transpose(bank[c][0:cn, s * P:(s + 1) * P], text[:, par, s, c0:c0 + cn], ident[:, :])
                    last.then_inc(text_t_filled, 1)
                pe.wait_ge(ip_probs_ready, b + 1)
                for s in range(ST):
                    last = nc.tensor.transpose(bank[NC][0:HIP, s * P:(s + 1) * P], ip_probs[:, par, s, :], ident[:, :])
                last.then_inc(text_t_filled, 1)

            def project(b, par, free):
                pe.wait_ge(text_t_ready, (NC + 1) * (b + 1))
                for s in range(ST):
                    if free:
                        pe.wait_ge(y_ready, ST * (b - 1) + s + 1)
                    y = bank[4 + s][:, 0:C]
                    for c, (c0, cn) in enumerate(CT):
                        nc.tensor.matmul(y, text_t[0:cn, par, c, s * P:(s + 1) * P], wout[0:cn, c, :], start=(c == 0), stop=False)
                    nc.tensor.matmul(y, ip_probs_t[0:HIP + 1, par, s * P:(s + 1) * P], vw[0:HIP + 1, b, :], start=False,
                                     stop=True).then_inc(y_filled, 1)

            pe.wait_ge(late_loaded, 16 * (1 + B))
            pe.wait_ge(vw_ready, B)
            text_transposes(0, 0, False)
            text_transposes(1, 1, True)
            project(0, 0, False)
            with pe.Fori(1, B // 2) as pair:
                text_transposes(2 * pair, 0, True)
                project(2 * pair - 1, 1, True)
                text_transposes(2 * pair + 1, 1, True)
                project(2 * pair, 0, True)
            project(B - 1, 1, True)


INPUTS = ["x", "ctx_2048", "fside_S_0", "L0_xattn_W_q", "L0_xattn_W_k", "L0_xattn_W_v", "L0_xattn_W_k_ip",
          "L0_xattn_W_v_ip", "L0_xattn_W_out", "L0_xattn_b_out"]


def kernel(**inputs):
    import numpy as np
    import concourse.bacc as bacc
    from concourse import mybir
    from concourse.bass_utils import run_bass_kernel_spmd

    nc = bacc.Bacc("TRN2", target_bir_lowering=False, num_devices=1)
    arrays, args = {}, []
    for name in INPUTS:
        a = np.ascontiguousarray(inputs[name])
        arrays[f"in_{name}"] = a
        args.append(nc.dram_tensor(f"in_{name}", a.shape, mybir.dt.from_np(a.dtype), kind="ExternalInput").ap())
    args.append(nc.dram_tensor("result", inputs["x"].shape, mybir.dt.float32, kind="ExternalOutput").ap())
    xattn_kernel(nc, *args)
    r = run_bass_kernel_spmd(nc, [arrays], core_ids=[0])
    return r.results[0]["result"]
```
